# Optimizing a Trainium2 kernel written in Bass

```python
import numpy as np
import jax
import jax.numpy as jnp

def _softmax(x, axis=-1):
    return jax.nn.softmax(x, axis=axis)

def _gelu(x):
    return jax.nn.gelu(x, approximate=True)

def _silu(x):
    return jax.nn.silu(x)

def _sigmoid(x):
    return jax.nn.sigmoid(x)

def _layernorm(x, axis=-1, eps=1e-05):
    m = jnp.mean(x, axis=axis, keepdims=True)
    v = jnp.var(x, axis=axis, keepdims=True)
    return (x - m) / jnp.sqrt(v + eps)

def _scatter_add(tgt, idx, src, axis=0):
    return tgt.at[idx].add(src)

def _segment_sum(src, seg, n):
    return jax.ops.segment_sum(src, seg, n)
kernel_name = 'mk_prb_d1_jaxref_r8_4fb7e9'

def setup_inputs(seed: int=0):
    np.random.seed(seed)
    _w = jnp.asarray

    def _L0_attn_setup():
        import jax, jax.numpy as jnp
        import numpy as np
        DIM = 128
        HEADS = 16
        DIM_HEAD = 64
        NUM_FREQS = 16
        INNER = HEADS * DIM_HEAD

        def rotate_half(x):
            x1 = x[..., ::2]
            x2 = x[..., 1::2]
            return jnp.concatenate((-x2, x1), axis=-1)

        def rope_fourier_cache(seq_len, head_dim, num_freqs):
            freqs = 10000.0 ** (-jnp.arange(0, head_dim, 2, dtype=jnp.float32) / head_dim)
            pos = jnp.arange(seq_len, dtype=jnp.float32)[:, None]
            angles = pos * freqs
            sin = jnp.sin(angles)
            cos = jnp.cos(angles)
            sin = jnp.stack([sin, sin], axis=-1).reshape(seq_len, head_dim)
            cos = jnp.stack([cos, cos], axis=-1).reshape(seq_len, head_dim)
            ffreqs = jnp.arange(1, num_freqs + 1, dtype=jnp.float32)
            p = jnp.arange(seq_len, dtype=jnp.float32)[:, None]
            fourier = jnp.concatenate([jnp.sin(p * ffreqs), jnp.cos(p * ffreqs)], axis=-1)
            return (sin, cos, fourier)
        key = jax.random.key(seed)
        ks = jax.random.split(key, 6)
        b, n = (4, 256)
        x = jax.random.normal(ks[0], (b, n, DIM), dtype=jnp.float32)
        w_qkv = jax.random.normal(ks[1], (3 * INNER, DIM), dtype=jnp.float32) * DIM ** (-0.5)
        w_fproj = jax.random.normal(ks[2], (DIM_HEAD, 2 * NUM_FREQS), dtype=jnp.float32) * (2 * NUM_FREQS) ** (-0.5)
        b_fproj = jax.random.normal(ks[3], (DIM_HEAD,), dtype=jnp.float32) * 0.02
        w_out = jax.random.normal(ks[4], (DIM, INNER), dtype=jnp.float32) * INNER ** (-0.5)
        b_out = jax.random.normal(ks[5], (DIM,), dtype=jnp.float32) * 0.02
        return {'x': x, 'w_qkv': w_qkv, 'w_fproj': w_fproj, 'b_fproj': b_fproj, 'w_out': w_out, 'b_out': b_out}
    _L0_attn_in = _L0_attn_setup()

    def _L0_ffn_setup():
        import math
        import jax, jax.numpy as jnp
        import numpy as np
        D_MODEL = 128
        D_HIDDEN = 256
        N_EXPERTS = 8
        TOP_K = 2
        CAPACITY_FACTOR = 1.25

        def _moe_forward(x, w_router, w_gate, w_down):
            B, T, D = x.shape
            N = B * T
            xf = x.reshape(N, D)
            logits = xf.astype(jnp.float32) @ w_router.T
            gates = jax.nn.softmax(logits, axis=-1)
            topk_gates, topk_idx = jax.lax.top_k(gates, TOP_K)
            expert_mask = jax.nn.one_hot(topk_idx, N_EXPERTS, dtype=jnp.int32).sum(axis=1)
            capacity = math.ceil(N / N_EXPERTS * CAPACITY_FACTOR)
            position_in_expert = jnp.cumsum(expert_mask, axis=0) - 1
            expert_mask = expert_mask * (position_in_expert < capacity)
            keep = jnp.take_along_axis(expert_mask, topk_idx, axis=1) > 0
            topk_gates = topk_gates * keep
            topk_gates = topk_gates / (topk_gates.sum(axis=-1, keepdims=True) + 1e-06)
            hidden = jax.nn.silu(xf @ w_gate.T)
            combine = (topk_gates[:, :, None] * jax.nn.one_hot(topk_idx, N_EXPERTS, dtype=topk_gates.dtype)).sum(axis=1)
            y = jnp.zeros((N, D), dtype=x.dtype)
            for e in range(N_EXPERTS):
                y = y + combine[:, e:e + 1] * (hidden @ w_down[e].T)
            return y.reshape(B, T, D)
        key = jax.random.key(seed)
        k0, k1, k2, k3 = jax.random.split(key, 4)
        B, T = (2, 256)
        x = jax.random.normal(k0, (B, T, D_MODEL), dtype=jnp.float32)
        w_router = jax.random.normal(k1, (N_EXPERTS, D_MODEL), dtype=jnp.float32) * 0.02
        w_gate = jax.random.normal(k2, (D_HIDDEN, D_MODEL), dtype=jnp.float32) * 0.02
        w_down = jax.random.normal(k3, (N_EXPERTS, D_MODEL, D_HIDDEN), dtype=jnp.float32) * 0.02
        return {'x': x, 'w_router': w_router, 'w_gate': w_gate, 'w_down': w_down}
    _L0_ffn_in = _L0_ffn_setup()
    _d = {'L0_attn_x': _L0_attn_in['x'], 'L0_attn_w_qkv': _L0_attn_in['w_qkv'], 'L0_attn_w_fproj': _L0_attn_in['w_fproj'], 'L0_attn_b_fproj': _L0_attn_in['b_fproj'], 'L0_attn_w_out': _L0_attn_in['w_out'], 'L0_attn_b_out': _L0_attn_in['b_out'], 'L0_ffn_w_router': _L0_ffn_in['w_router'], 'L0_ffn_w_gate': _L0_ffn_in['w_gate'], 'L0_ffn_w_down': _L0_ffn_in['w_down']}
    _x0 = _d['L0_attn_x']
    _d['L0_attn_x'] = jax.random.normal(jax.random.fold_in(jax.random.key(seed), 1), (1, 2048, 128), dtype=_x0.dtype)
    del _x0
    return _d

def reference(L0_attn_x, L0_attn_w_qkv, L0_attn_w_fproj, L0_attn_b_fproj, L0_attn_w_out, L0_attn_b_out, L0_ffn_w_router, L0_ffn_w_gate, L0_ffn_w_down):

    def _L0_attn_ref(x, w_qkv, w_fproj, b_fproj, w_out, b_out):
        import jax, jax.numpy as jnp
        import numpy as np
        DIM = 128
        HEADS = 16
        DIM_HEAD = 64
        NUM_FREQS = 16
        INNER = HEADS * DIM_HEAD

        def rotate_half(x):
            x1 = x[..., ::2]
            x2 = x[..., 1::2]
            return jnp.concatenate((-x2, x1), axis=-1)

        def rope_fourier_cache(seq_len, head_dim, num_freqs):
            freqs = 10000.0 ** (-jnp.arange(0, head_dim, 2, dtype=jnp.float32) / head_dim)
            pos = jnp.arange(seq_len, dtype=jnp.float32)[:, None]
            angles = pos * freqs
            sin = jnp.sin(angles)
            cos = jnp.cos(angles)
            sin = jnp.stack([sin, sin], axis=-1).reshape(seq_len, head_dim)
            cos = jnp.stack([cos, cos], axis=-1).reshape(seq_len, head_dim)
            ffreqs = jnp.arange(1, num_freqs + 1, dtype=jnp.float32)
            p = jnp.arange(seq_len, dtype=jnp.float32)[:, None]
            fourier = jnp.concatenate([jnp.sin(p * ffreqs), jnp.cos(p * ffreqs)], axis=-1)
            return (sin, cos, fourier)
        b, n, _ = x.shape
        scale = DIM_HEAD ** (-0.5)
        qkv = x @ w_qkv.T
        q, k, v = jnp.split(qkv, 3, axis=-1)

        def to_heads(t):
            return t.reshape(b, n, HEADS, DIM_HEAD).transpose(0, 2, 1, 3)
        q, k, v = (to_heads(q), to_heads(k), to_heads(v))
        sin, cos, fourier = rope_fourier_cache(n, DIM_HEAD, NUM_FREQS)
        fenc = fourier @ w_fproj.T + b_fproj
        fenc = fenc[None, None]
        q = q * cos + rotate_half(q) * sin + fenc
        k = k * cos + rotate_half(k) * sin + fenc
        dots = jnp.einsum('bhid,bhjd->bhij', q, k) * scale
        attn = jax.nn.softmax(dots, axis=-1)
        out = jnp.einsum('bhij,bhjd->bhid', attn, v)
        out = out.transpose(0, 2, 1, 3).reshape(b, n, INNER)
        return out @ w_out.T + b_out

    def _L0_ffn_ref(x, w_router, w_gate, w_down):
        import math
        import jax, jax.numpy as jnp
        import numpy as np
        D_MODEL = 128
        D_HIDDEN = 256
        N_EXPERTS = 8
        TOP_K = 2
        CAPACITY_FACTOR = 1.25

        def _moe_forward(x, w_router, w_gate, w_down):
            B, T, D = x.shape
            N = B * T
            xf = x.reshape(N, D)
            logits = xf.astype(jnp.float32) @ w_router.T
            gates = jax.nn.softmax(logits, axis=-1)
            topk_gates, topk_idx = jax.lax.top_k(gates, TOP_K)
            expert_mask = jax.nn.one_hot(topk_idx, N_EXPERTS, dtype=jnp.int32).sum(axis=1)
            capacity = math.ceil(N / N_EXPERTS * CAPACITY_FACTOR)
            position_in_expert = jnp.cumsum(expert_mask, axis=0) - 1
            expert_mask = expert_mask * (position_in_expert < capacity)
            keep = jnp.take_along_axis(expert_mask, topk_idx, axis=1) > 0
            topk_gates = topk_gates * keep
            topk_gates = topk_gates / (topk_gates.sum(axis=-1, keepdims=True) + 1e-06)
            hidden = jax.nn.silu(xf @ w_gate.T)
            combine = (topk_gates[:, :, None] * jax.nn.one_hot(topk_idx, N_EXPERTS, dtype=topk_gates.dtype)).sum(axis=1)
            y = jnp.zeros((N, D), dtype=x.dtype)
            for e in range(N_EXPERTS):
                y = y + combine[:, e:e + 1] * (hidden @ w_down[e].T)
            return y.reshape(B, T, D)
        return _moe_forward(x, w_router, w_gate, w_down)
    x = L0_attn_x
    xn = _layernorm(x, axis=-1)
    x = x + _L0_attn_ref(xn, L0_attn_w_qkv, L0_attn_w_fproj, L0_attn_b_fproj, L0_attn_w_out, L0_attn_b_out) + _L0_ffn_ref(xn, L0_ffn_w_router, L0_ffn_w_gate, L0_ffn_w_down)
    return x

_drawn_inputs = setup_inputs


def setup_inputs(seed=0):
    import zlib

    import numpy as np

    out = dict(_drawn_inputs(seed))
    spreads = {}
    factors = {'L0_attn_b_fproj': 8.0, 'L0_ffn_w_router': 8.529}
    for name, (base, spread) in spreads.items():
        noise = np.random.default_rng([zlib.crc32(name.encode()), seed]).standard_normal(out[name].shape)
        drawn = base * np.exp(spread * noise) if base else spread * noise
        out[name] = jnp.asarray(drawn.astype(out[name].dtype))
    for name, factor in factors.items():
        out[name] = (out[name] * factor).astype(out[name].dtype)
    return out
```

```python
from contextlib import ExitStack

import concourse.bass as bass
import numpy as np
from concourse import mybir

F32 = mybir.dt.float32
F32R = mybir.dt.float32r
ALU = mybir.AluOpType
ACT = mybir.ActivationFunctionType
AX = mybir.AxisListType

P = 128
N = 2048
D = 128
HEADS = 16
DH = 64
PAIRS = HEADS // 2
BLOCKS = N // P
CHUNK = 512
CHUNKS = N // CHUNK
PER = CHUNK // P
STEPS = CHUNKS * BLOCKS
FREQS = 16
HIDDEN = 256
EXPERTS = 8
TOP_K = 2
CAPACITY = -(-N * 5 // (EXPERTS * 4))
EPS = 1e-5
SCALE = DH ** -0.5

EXP_SLOTS = 4
SUM_POOL = (256, 512, 896, 896)
WINDOWS = 5
WINDOW_ORDER = (2, 3, 0, 1, 4)
QA, QB, KA, KB = 0, 1, 2, 3

READER = {"qk": "dve", "max": "dve", "den": "dve", "proj": "dve", "logit": "dve", "count": "dve",
          "v": "act", "window": "act", "mt": "act", "hidden": "act", "xt": "act", "fenc": "act"}


PREP_STRIDE = 6
ROPE_AT, HIGH_AT, LOW_AT, VALUES_AT, WINDOWS_AT = 2, (4, 4, 5), 5, 6, 7
MAX_FROM, MAX_TO = 11, 60
MT_STEP = 62
DEN_AT, INVERT_AT, NORMALISE_AT, PROJ_AT = 2, 3, 4, 8
BOX = 32


def vector_load(n):
    load = 1.9 * (1 - SUM_POOL[n // BLOCKS] / (2 * CHUNK))
    if n < PREP_STRIDE * CHUNKS:
        load += 3 * (n % PREP_STRIDE < 2) + 2 * (n % PREP_STRIDE == LOW_AT)
    load += n % BLOCKS in (DEN_AT, INVERT_AT, NORMALISE_AT, PROJ_AT)
    return load


def prep_events(steps):
    for c in range(CHUNKS):
        b = PREP_STRIDE * c
        steps[b].append(("qk", c, 0))
        steps[b + 1].append(("qk", c, 1))
        steps[b + VALUES_AT].append(("v", c))
        for at, w in enumerate(WINDOW_ORDER):
            steps[b + WINDOWS_AT + at].append(("window", c, w))
    todo = [("max", h, i, j) for c in range(CHUNKS) for i in range(BLOCKS) for h in range(2)
            for j in range(CHUNKS) if max(i // PER, j) == c]
    load = [vector_load(n) for n in range(STEPS)]
    for n in range(MAX_FROM, MAX_TO + 1):
        share = (len(todo) + sum(load[n:MAX_TO + 1])) / (MAX_TO + 1 - n) - load[n]
        for _ in range(round(share)):
            if not todo:
                break
            chunk = max(todo[0][2] // PER, todo[0][3])
            if n < PREP_STRIDE * chunk + WINDOWS_AT + WINDOWS - 1:
                break
            steps[n].append(todo.pop(0))
    assert not todo
    steps[MT_STEP].append(("mt",))


class Body:

    def __init__(self, pair, main, carry, prep, extra=(), before=None, pair_stride=0):
        self.pair, self.main, self.carry, self.prep = pair, main, carry, prep
        self.pair_stride = pair_stride
        steps = [[] for _ in range(STEPS)]
        if carry:
            steps[DEN_AT].append(("den", CHUNKS - 1))
            steps[PROJ_AT].append(("proj", CHUNKS - 1))
        if prep:
            prep_events(steps)
        if main:
            for c in range(CHUNKS - 1):
                steps[BLOCKS * (c + 1) + DEN_AT].append(("den", c))
                steps[BLOCKS * (c + 1) + PROJ_AT].append(("proj", c))
        for n, ev in extra:
            steps[n].append(ev)
        for evs in steps:
            evs.sort(key=lambda ev: READER[ev[0]] != "act")
        self.steps = steps
        self.order = [ev for evs in steps for ev in evs]
        self.before = before
        self.count = {"full": len(self.order),
                      "dve": sum(READER[ev[0]] == "dve" for ev in self.order),
                      "act": sum(READER[ev[0]] == "act" for ev in self.order)}
        self.start = {s: before.start[s] + before.count[s] if before else 0 for s in self.count}
        self.stride = {s: 0 for s in self.count}

    def index(self, ev):
        return self.order.index(ev)

    def bank(self, i):
        return (i - len(self.order)) % 3

    def full(self, i):
        return "full", i + 1

    def read(self, i):
        r = READER[self.order[i][0]]
        return r, sum(READER[ev[0]] == r for ev in self.order[:i + 1])

    def last_user(self, i):
        if i >= 3:
            return self.read(i - 3)
        if self.before is None:
            return None
        bank = self.bank(i)
        back = (-bank) % 3 or 3
        tail = self.before.order[-back:]
        if len(tail) < back:
            return None
        r = READER[tail[0][0]]
        return r, -sum(READER[ev[0]] == r for ev in tail[1:])


def attention_and_mixture(nc, x_in, w_qkv, w_fproj, w_out, b_out, w_router, w_gate, w_down,
                          cos_in, sin_in, fourier, ident_in, tri_in, lower_in, out):
    with ExitStack() as ctx:
        def sb(name, shape, dt=F32):
            return ctx.enter_context(nc.sbuf_tensor(name, shape, dt))

        def sem(name):
            return ctx.enter_context(nc.semaphore(name))

        q1 = [[sb(f"q1_{s}{h}", [P, N], F32R) for h in range(2)] for s in range(2)]
        k1 = [[sb(f"k1_{s}{h}", [P, N], F32R) for h in range(2)] for s in range(2)]
        k2 = [[sb(f"k2_{s}{h}", [P, N], F32R) for h in range(2)] for s in range(2)]
        q2 = [[sb(f"q2_{s}{h}", [P, CHUNK], F32R) for h in range(2)] for s in range(2)]
        v = [sb(f"v_{s}", [P, BLOCKS, P]) for s in range(2)]
        xnT = sb("xnT", [P, N])
        acc = sb("acc", [P, BLOCKS, D])
        wp = [sb(f"wp_{s}", [P, 3 * P]) for s in range(2)]
        wo = [sb(f"wo_{s}", [P, D]) for s in range(2)]
        cos = sb("cos", [P, BLOCKS, DH])
        sin = sb("sin", [P, BLOCKS, DH])
        fenc = sb("fenc", [P, BLOCKS, DH])
        tu = sb("tu", [P, 2, PER, 4, DH])
        split = sb("split", [P, PER, WINDOWS * P])
        probs = sb("probs", [P, EXP_SLOTS, 2 * CHUNK])
        sums = sb("sums", [P, 2, 2 * CHUNK])
        ob = sb("ob", [P, 2, CHUNK])
        mparts = sb("mparts", [P, 2 * BLOCKS, CHUNKS])
        mneg = sb("mneg", [P, 2 * BLOCKS])
        mrow = sb("mrow", [2 * BLOCKS, P], F32R)
        ident = sb("ident", [P, P])
        ones = sb("ones", [P, P])
        tri = sb("tri", [P, P])
        lower = sb("lower", [P, EXPERTS * EXPERTS])
        wf = sb("wf", [2 * FREQS + 1, DH])
        wr = sb("wr", [P, EXPERTS])
        wg = sb("wg", [P, HIDDEN])
        bo = sb("bo", [P, D])
        stats = sb("stats", [P, 5, BLOCKS])
        inverse = sb("inverse", [P, CHUNK // BOX])

        o_raw, o_norm = ob[:, 0, :], ob[:, 1, :]
        t_rope, u_rope = tu[:, 0], tu[:, 1]
        split_r = split[:, :, :].bitcast(F32R)
        hT = probs[:, :, :].rearrange("p a b -> p (a b)").rearrange("p (k n) -> p k n", k=2)
        wd = v[1][:, :, :].rearrange("p a b -> p (a b)").rearrange("p (k n) -> p k n", k=2)
        fourT = v[0][:, :, :].rearrange("p a b -> p (a b)")
        xc = sums[:, :, :].rearrange("p a b -> p (a b)").rearrange("p (b d) -> p b d", d=D)
        squares = tu[:, :, :, :, :].rearrange("p a b c d -> p (a b c d)")
        beats = sums[:, 0, :].rearrange("p (b e f) -> p b e f", e=EXPERTS, f=EXPERTS)
        ties = sums[:, 1, :].rearrange("p (b e f) -> p b e f", e=EXPERTS, f=EXPERTS)
        small = ob[:, :, :].rearrange("p a (s b e) -> p (a s) b e", s=4, e=EXPERTS)
        logits, gates, rank, mask, upto, place, comb = (small[:, i] for i in range(7))

        psum = [ctx.enter_context(nc.psum_tensor(f"scores_{i}", [P, 2 * CHUNK], F32)) for i in range(2)]
        ring = [ctx.enter_context(nc.psum_tensor(f"ring_{i}", [P, CHUNK], F32)) for i in range(3)]
        oT = ctx.enter_context(nc.psum_tensor("oT", [P, CHUNK], F32))

        x_here = [sem(f"x_here{c}") for c in range(CHUNKS)]
        ident_here, tables_here, four_here = sem("ident_here"), sem("tables_here"), sem("four_here")
        router_here, gate_here, down_here = sem("router_here"), sem("gate_here"), sem("down_here")
        bo_here = sem("bo_here")
        wp_here = [sem(f"wp_here{s}") for s in range(2)]
        wo_here = [sem(f"wo_here{s}") for s in range(2)]
        q2_here = [sem(f"q2_here{s}") for s in range(2)]
        out_there = sem("out_there")
        consts_set = sem("consts_set")
        dve_chain = sem("dve_chain")
        squared, root_taken, xn_ready = sem("squared"), sem("root_taken"), sem("xn_ready")
        var_ready = sem("var_ready")
        exped_gates, mask_ready, comb_ready = sem("exped_gates"), sem("mask_ready"), sem("comb_ready")
        experts_done, weighted, mixture_added = sem("experts_done"), sem("weighted"), sem("mixture_added")
        pool_chain = sem("pool_chain")
        ring_sem = {"full": sem("ring_full"), "dve": sem("ring_read_dve"), "act": sem("ring_read_act")}
        roped, high_done, low_done, mneg_ready = sem("roped"), sem("high_done"), sem("low_done"), sem("mneg_ready")
        scores_done, exp_done, values_done = sem("scores_done"), sem("exp_done"), sem("values_done")
        summed_dve, summed_pool = sem("summed_dve"), sem("summed_pool")
        o_copied, inverted, o_ready = sem("o_copied"), sem("inverted"), sem("o_ready")

        pre = Body(-1, False, False, False,
                   extra=[(0, ("fenc", 0)), (1, ("fenc", 1))] + [(2 + c, ("xt", c)) for c in range(CHUNKS)])
        first = Body(-1, False, False, True, before=pre, extra=
                     [(3, ("logit",))] + [(4 + i + 2 * (i > 3), ("hidden", i % 2, i // 2)) for i in range(8)]
                     + [(19, ("count",))])
        Y_AT = {26 + 2 * b: b for b in range(BLOCKS)}
        b0 = Body(0, True, False, True, before=first)
        odd = Body(1, True, True, True, before=b0, pair_stride=2)
        even = Body(2, True, True, True, before=odd, pair_stride=2)
        ROUNDS = (PAIRS - 2) // 2
        for b in (odd, even):
            b.stride = {s: odd.count[s] + even.count[s] for s in b.count}
        last = Body(PAIRS - 1, True, True, False, before=even)
        last.start = {s: odd.start[s] + ROUNDS * odd.stride[s] for s in odd.start}
        tail = Body(PAIRS, False, True, False, before=last)

        def pair_count(b, per, local, k):
            base = per * b.pair + local
            return base if k is None or not b.pair_stride else k * (per * b.pair_stride) + base

        def wait_pair(eng, s, b, per, local, k):
            if k is not None or per * b.pair + local > 0:
                eng.wait_ge(s, pair_count(b, per, local, k))

        def wait_ring(eng, b, what, k):
            if what is None:
                return
            s, local = what
            base = b.start[s] + local
            if k is not None or base > 0:
                eng.wait_ge(ring_sem[s], base if k is None else k * b.stride[s] + base)

        def sum_count(n):
            return (BLOCKS - 1) * (n // BLOCKS) + max(n % BLOCKS, 1)

        block = ctx.enter_context(nc.Block())

        @block.sync
        def _(sp):
            def load(dst, src, s):
                sp.dma_start(dst, src).then_inc(s, 16)

            def pair_loads(b, k):
                s = b.pair % 2
                pair = b.pair + (0 if k is None else k * b.pair_stride)
                if b.main:
                    wait_pair(sp, scores_done, b, STEPS, 0, k)
                    query_chunk(s, 1)
                    if b.prep:
                        load(wp[s][:, :], w_qkv[pair + 2], wp_here[s])
                    wait_pair(sp, scores_done, b, STEPS, BLOCKS + 1, k)
                    query_chunk(s, 2)
                    if b.prep:
                        load(wo[1 - s][:, :], w_out[pair + 1], wo_here[1 - s])
                    wait_pair(sp, scores_done, b, STEPS, 2 * BLOCKS, k)
                    query_chunk(s, 3)
                if b.prep:
                    wait_ring(sp, b, b.read(b.index(("mt",))), k)
                    query_chunk(1 - s, 0)

            def query_chunk(s, c):
                at = slice(c * CHUNK, (c + 1) * CHUNK)
                for h, q_rows, m_row in ((0, slice(0, DH), slice(DH, DH + 1)), (1, slice(DH, P), slice(0, 1))):
                    to = q2[c % 2][h]
                    first_block = BLOCKS * h + PER * c
                    load(to[q_rows, :].bitcast(F32), q1[s][h][q_rows, at].bitcast(F32), q2_here[c % 2])
                    load(to[m_row, :].bitcast(F32), mrow[first_block:first_block + PER, :].bitcast(F32),
                         q2_here[c % 2])

            for c in range(CHUNKS):
                load(acc[:, PER * c:PER * (c + 1), :], x_in[:, PER * c:PER * (c + 1), :], x_here[c])
            load(ident[:, :], ident_in, ident_here)
            load(wp[0][:, :], w_qkv[0], wp_here[0])
            load(wr[:, :], w_router, router_here)
            load(wg[:, :], w_gate, gate_here)
            load(wd, w_down, down_here)
            load(wp[1][:, :], w_qkv[1], wp_here[1])
            load(wo[0][:, :], w_out[0], wo_here[0])
            sp.wait_ge(consts_set, 1)
            pair_loads(first, None)
            pair_loads(b0, None)
            with sp.Fori(0, ROUNDS) as k:
                pair_loads(odd, k)
                pair_loads(even, k)
            pair_loads(last, None)
            for c in range(CHUNKS):
                b = last if c < CHUNKS - 1 else tail
                wait_ring(sp, b, b.read(b.index(("proj", c))), None)
                load(out[:, PER * c:PER * (c + 1), :], acc[:, PER * c:PER * (c + 1), :], out_there)
            sp.wait_ge(out_there, 16 * CHUNKS)

        @block.tensor
        def _(pe):
            def mm(o, l, r, start=True, stop=True, **more):
                return pe.matmul(o, l, r, start=start, stop=stop, skip_group_check=True, **more)

            def scores(b, n, h, k):
                c, j, s = n // BLOCKS, n % BLOCKS, b.pair % 2
                if n == 0 and h == 0:
                    wait_ring(pe, b, ("act", 0), k)
                    if b.pair == 0:
                        pe.wait_ge(weighted, BLOCKS)
                if j == 0 and h == 0:
                    wait_pair(pe, q2_here[c % 2], b, 128, 64 * (c // 2 + 1), k)
                if h == 0:
                    wait_pair(pe, exp_done, b, STEPS, n - 1, k)
                keys, queries = slice(P * j, P * (j + 1)), slice(CHUNK * c, CHUNK * (c + 1))
                o = psum[n % 2][:, CHUNK * h:CHUNK * (h + 1)]
                mm(o, k1[s][h][:, keys], q1[s][h][:, queries], stop=False)
                last_mm = mm(o, k2[s][h][:, keys], q2[c % 2][h][:, :], start=False)
                if h == 1:
                    last_mm.then_inc(scores_done, 1)

            def values(b, n, k):
                j, s = n % BLOCKS, (b.pair + (n < 0)) % 2
                wait_pair(pe, exp_done, b, STEPS, n + 1, k)
                if j == 0:
                    wait_pair(pe, o_copied, b, CHUNKS, n // BLOCKS, k)
                for h in range(2):
                    last_mm = mm(oT[DH * h:DH * (h + 1), :], v[s][:, j, DH * h:DH * (h + 1)],
                                 probs[:, n % EXP_SLOTS, CHUNK * h:CHUNK * (h + 1)],
                                 start=(j == 0), stop=(j == BLOCKS - 1))
                last_mm.then_inc(values_done, 1)

            def fill(b, ev, seen, k):
                i = b.index(ev)
                bank = ring[b.bank(i)]
                wait_ring(pe, b, b.last_user(i), k)
                kind = ev[0]
                s = (b.pair + 1) % 2
                if kind == "qk":
                    _, c, f = ev
                    if c == 0 and f == 0:
                        wait_pair(pe, wp_here[s], b, 8, 24 if s == 0 else 16, k)
                    for g in range(2):
                        t = PER * c + 2 * f + g
                        last_mm = mm(bank[:, 2 * P * g:2 * P * (g + 1)], xnT[:, P * t:P * (t + 1)],
                                     wp[s][:, 0:2 * P])
                elif kind == "v":
                    for g in range(PER):
                        t = PER * ev[1] + g
                        last_mm = mm(bank[:, P * g:P * (g + 1)], xnT[:, P * t:P * (t + 1)], wp[s][:, 2 * P:3 * P])
                elif kind == "window":
                    _, c, w = ev
                    if w == WINDOW_ORDER[0]:
                        wait_pair(pe, high_done, b, CHUNKS, CHUNKS + c + 1, k)
                    if w == 0:
                        wait_pair(pe, low_done, b, CHUNKS, CHUNKS + c + 1, k)
                    for g in range(PER):
                        last_mm = pe.transpose(bank[:, P * g:P * (g + 1)], split[:, g, P * w:P * (w + 1)],
                                               ident[:, :])
                elif kind == "max":
                    _, h, i_, j = ev
                    need = b.read(b.index(("window", max(i_ // PER, j), 1)))
                    if need not in seen:
                        wait_ring(pe, b, need, k)
                        seen.append(need)
                    last_mm = mm(bank[:, :], q1[s][h][:, P * i_:P * (i_ + 1)], k1[s][h][:, CHUNK * j:CHUNK * (j + 1)])
                elif kind == "mt":
                    wait_pair(pe, mneg_ready, b, 1, 2, k)
                    last_mm = pe.transpose(bank[0:2 * BLOCKS, 0:P], mneg[:, :], ident[:, :])
                elif kind == "den":
                    g = ev[1] + (-CHUNKS if b.carry and ev[1] == CHUNKS - 1 else 0)
                    for q in (summed_dve, summed_pool):
                        wait_pair(pe, q, b, CHUNKS * (BLOCKS - 1), (BLOCKS - 1) * (g + 1), k)
                    for h in range(2):
                        last_mm = mm(bank[DH * h:DH * (h + 1), :], ones[:, 0:DH],
                                     sums[:, ev[1] % 2, CHUNK * h:CHUNK * (h + 1)])
                elif kind == "proj":
                    g = ev[1] + (-CHUNKS if b.carry and ev[1] == CHUNKS - 1 else 0)
                    s = (b.pair + (g < 0)) % 2
                    if ev[1] == 0 and b.main:
                        wait_pair(pe, wo_here[s], b, 8, 16 if s == 0 else 8, k)
                    wait_pair(pe, o_ready, b, CHUNKS, g + 1, k)
                    for t in range(PER):
                        last_mm = mm(bank[:, P * t:P * (t + 1)], o_norm[:, P * t:P * (t + 1)], wo[s][:, :])
                elif kind == "xt":
                    pe.wait_ge(xn_ready, ev[1] + 1)
                    if ev[1] == 0:
                        pe.wait_ge(ident_here, 16)
                    for g in range(PER):
                        last_mm = pe.transpose(bank[:, P * g:P * (g + 1)], xc[:, PER * ev[1] + g, :], ident[:, :])
                elif kind == "fenc":
                    pe.wait_ge(four_here, 32)
                    for g in range(8):
                        t = 8 * ev[1] + g
                        last_mm = mm(bank[:, DH * g:DH * (g + 1)], fourT[0:2 * FREQS + 1, P * t:P * (t + 1)], wf[:, :])
                elif kind == "logit":
                    pe.wait_ge(router_here, 16)
                    for t in range(BLOCKS):
                        last_mm = mm(bank[:, EXPERTS * t:EXPERTS * (t + 1)], xnT[:, P * t:P * (t + 1)], wr[:, :])
                elif kind == "hidden":
                    pe.wait_ge(gate_here, 16)
                    last_mm = mm(bank[:, :], wg[:, P * ev[1]:P * (ev[1] + 1)], xnT[:, CHUNK * ev[2]:CHUNK * (ev[2] + 1)])
                elif kind == "count":
                    pe.wait_ge(mask_ready, 1)
                    pe.wait_ge(consts_set, 1)
                    flat = mask.rearrange("p b e -> p (b e)")
                    mm(bank[:, 0:P], tri[:, :], flat)
                    last_mm = mm(bank[:, P:2 * P], ones[:, :], flat)
                last_mm.then_inc(ring_sem["full"], 1)

            def experts(b, t):
                if t == 0:
                    pe.wait_ge(down_here, 16)
                    wait_ring(pe, b, b.read(b.index(("hidden", 1, CHUNKS - 1))), None)
                if t >= 2:
                    pe.wait_ge(weighted, t - 1)
                for half in range(2):
                    for q in range(2):
                        last_mm = mm(psum[t % 2][:, CHUNK * half:CHUNK * (half + 1)], hT[:, q, P * t:P * (t + 1)],
                                     wd[:, q, CHUNK * half:CHUNK * (half + 1)], start=(q == 0), stop=(q == 1))
                last_mm.then_inc(experts_done, 1)

            def body(b, k=None):
                seen = []
                for n in range(STEPS):
                    mine = [ev for ev in b.steps[n] if READER[ev[0]] == "act"]
                    rest = [ev for ev in b.steps[n] if READER[ev[0]] != "act"]
                    third = -(-len(rest) // 3)
                    for ev in mine:
                        fill(b, ev, seen, k)
                    for part in range(3):
                        if b.main and part < 2:
                            scores(b, n, part, k)
                        if part == 2 and ((b.main and n > 0) or (b.carry and n == 0)):
                            values(b, n - 1, k)
                        for ev in rest[third * part:third * (part + 1)]:
                            fill(b, ev, seen, k)
                    if b is first and n in Y_AT:
                        experts(b, Y_AT[n])

            body(pre)
            wait_ring(pe, first, ("act", 0), None)
            body(first)
            body(b0)
            with pe.Fori(0, ROUNDS) as k:
                body(odd, k)
                body(even, k)
            body(last)
            body(tail)

        @block.scalar
        def _(act):
            def read(b, ev, k):
                if READER[ev[0]] != "act":
                    return
                i = b.index(ev)
                bank = ring[b.bank(i)]
                s = (b.pair + 1) % 2
                kind = ev[0]
                if kind == "v" and ev[1] == 0:
                    wait_pair(act, values_done, b, STEPS, 0, k)
                wait_ring(act, b, b.full(i), k)
                if kind == "v":
                    c = ev[1]
                    ins = act.copy(v[s][:, PER * c:PER * (c + 1), :], bank[:, :])
                elif kind == "window":
                    _, c, w = ev
                    at = slice(CHUNK * c, CHUNK * (c + 1))
                    if w < 4:
                        ins = act.copy((q1, q1, k1, k1)[w][s][w % 2][:, at], bank[:, :])
                    else:
                        act.copy(k2[s][0][0:DH, at], bank[0:DH, :])
                        ins = act.copy(k2[s][1][DH:P, at], bank[DH:P, :])
                elif kind == "mt":
                    ins = act.copy(mrow[:, :], bank[0:2 * BLOCKS, 0:P])
                elif kind == "xt":
                    ins = act.copy(xnT[:, CHUNK * ev[1]:CHUNK * (ev[1] + 1)], bank[:, :])
                elif kind == "fenc":
                    ins = act.copy(fenc[:, 8 * ev[1]:8 * (ev[1] + 1), :], bank[:, :])
                elif kind == "hidden":
                    ins = act.activation(hT[:, ev[1], CHUNK * ev[2]:CHUNK * (ev[2] + 1)], bank[:, :], ACT.Silu)
                ins.then_inc(ring_sem["act"], 1)

            def exps(b, n, k):
                wait_pair(act, scores_done, b, STEPS, n + 1, k)
                wait_pair(act, values_done, b, STEPS, n - EXP_SLOTS + 1, k)
                for q in (summed_dve, summed_pool):
                    wait_pair(act, q, b, CHUNKS * (BLOCKS - 1), sum_count(n - EXP_SLOTS), k)
                act.activation(probs[:, n % EXP_SLOTS, :], psum[n % 2][:, :], ACT.Exp, scale=SCALE)\
                   .then_inc(exp_done, 1)

            def copy_output(b, g, k):
                wait_pair(act, values_done, b, STEPS, BLOCKS * (g + 1), k)
                wait_pair(act, o_ready, b, CHUNKS, g, k)
                act.copy(o_raw, oT[:, :]).then_inc(o_copied, 1)

            def high_parts(b, c, piece, k):
                if piece == 0:
                    wait_pair(act, roped, b, 2 * CHUNKS, 2 * (CHUNKS + c + 1), k)
                    q_out = split_r[:, :, 0:4 * DH].rearrange("p g (a d) -> p g a d", d=DH)[:, :, 0:4:3, :]
                    act.copy(q_out, t_rope[:, :, QA:KA, :])
                    return
                k_out = split_r[:, :, 4 * DH:8 * DH].rearrange("p g (a t d) -> p g a t d", t=2, d=DH)
                ins = act.copy(k_out[:, :, :, piece - 1, :], t_rope[:, :, KA:KB + 1, :])
                if piece == 2:
                    ins.then_inc(high_done, 1)

            def body(b, k=None):
                for n in range(STEPS):
                    if b is first and n == 7:
                        wait_ring(act, b, b.read(b.index(("logit",))), k)
                        act.activation(gates, logits, ACT.Exp).then_inc(exped_gates, 1)
                    for ev in b.steps[n]:
                        read(b, ev, k)
                    if b.main:
                        exps(b, n, k)
                    for piece, at in enumerate(HIGH_AT):
                        if b.prep and n % PREP_STRIDE == at and n < PREP_STRIDE * CHUNKS:
                            high_parts(b, n // PREP_STRIDE, piece, k)
                    if b.main and n % BLOCKS == 0 and n:
                        copy_output(b, n // BLOCKS - 1, k)
                    if b.carry and n == 0:
                        copy_output(b, -1, k)

            act.dma_start(fourT[0:2 * FREQS + 1, :], fourier).then_inc(four_here, 16)
            act.dma_start(wf[:, :], w_fproj).then_inc(four_here, 16)
            act.dma_start(cos[:, :, :], cos_in).then_inc(tables_here, 16)
            act.dma_start(sin[:, :, :], sin_in).then_inc(tables_here, 16)
            act.dma_start(tri[:, :], tri_in).then_inc(tables_here, 16)
            act.dma_start(lower[:, :], lower_in.to_broadcast([P, EXPERTS * EXPERTS])).then_inc(tables_here, 16)
            act.dma_start(bo[:, :], b_out.to_broadcast([P, D])).then_inc(bo_here, 16)
            for c in range(CHUNKS):
                act.wait_ge(squared, 2 * c + 1)
                act.activation(squares[:, CHUNK * c:CHUNK * (c + 1)], xc[:, PER * c:PER * (c + 1), :], ACT.Square)\
                   .then_inc(squared, 1)
            for c in range(CHUNKS):
                act.wait_ge(var_ready, c + 1)
                act.activation(stats[:, 3, PER * c:PER * (c + 1)], stats[:, 2, PER * c:PER * (c + 1)], ACT.Sqrt)\
                   .then_inc(root_taken, 1)
            body(pre)
            body(first)
            body(b0)
            with act.Fori(0, ROUNDS) as k:
                body(odd, k)
                body(even, k)
            body(last)
            body(tail)

        @block.vector
        def _(dve):
            chained = [0]

            def chain(ins):
                chained[0] += 1
                ins.then_inc(dve_chain, 1)
                dve.wait_ge(dve_chain, chained[0])

            def layernorm():
                for c in range(CHUNKS):
                    x, y = acc[:, PER * c:PER * (c + 1), :], xc[:, PER * c:PER * (c + 1), :]
                    st = [stats[:, i, PER * c:PER * (c + 1)] for i in range(5)]
                    dve.wait_ge(x_here[c], 16)
                    chain(dve.tensor_reduce(st[0], x, AX.X, ALU.add))
                    chain(dve.tensor_scalar(st[1], st[0], -1.0 / D, None, ALU.mult))
                    dve.tensor_tensor(y, x, st[1][:, :, None].to_broadcast([P, PER, D]), ALU.add).then_inc(squared, 1)
                    dve.wait_ge(squared, 2 * c + 2)
                    chain(dve.tensor_reduce(st[0], squares[:, CHUNK * c:CHUNK * (c + 1)].rearrange(
                        "p (b d) -> p b d", d=D), AX.X, ALU.add))
                    dve.tensor_scalar(st[2], st[0], 1.0 / D, EPS, ALU.mult, ALU.add).then_inc(var_ready, 1)
                for c in range(CHUNKS):
                    y = xc[:, PER * c:PER * (c + 1), :]
                    st = [stats[:, i, PER * c:PER * (c + 1)] for i in range(5)]
                    dve.wait_ge(root_taken, c + 1)
                    chain(dve.reciprocal(st[4], st[3]))
                    dve.tensor_tensor(y, y, st[4][:, :, None].to_broadcast([P, PER, D]), ALU.mult).then_inc(xn_ready, 1)

            def wide(t, axis):
                t = t[:, :, None, :] if axis == 2 else t[:, :, :, None]
                return t.to_broadcast([P, BLOCKS, EXPERTS, EXPERTS])

            def row(t):
                return t[:, :, None].to_broadcast([P, BLOCKS, EXPERTS])

            def choose():
                dve.wait_ge(exped_gates, 1)
                chain(dve.tensor_reduce(stats[:, 0, :], gates, AX.X, ALU.add))
                chain(dve.reciprocal(stats[:, 1, :], stats[:, 0, :]))
                chain(dve.tensor_tensor(gates, gates, row(stats[:, 1, :]), ALU.mult))
                dve.tensor_tensor(beats, wide(gates, 2), wide(gates, 3), ALU.is_gt)
                chain(dve.tensor_tensor(ties, wide(gates, 2), wide(gates, 3), ALU.is_equal))
                flat_ties = ties.rearrange("p b e f -> p b (e f)")
                chain(dve.tensor_tensor(flat_ties, flat_ties, lower[:, None, :].to_broadcast(
                    [P, BLOCKS, EXPERTS * EXPERTS]), ALU.mult))
                chain(dve.tensor_tensor(beats, beats, ties, ALU.add))
                chain(dve.tensor_reduce(rank, beats, AX.X, ALU.add))
                dve.tensor_scalar(mask, rank, float(TOP_K), None, ALU.is_lt).then_inc(mask_ready, 1)

            def keep(b, i, bank):
                within = bank[:, 0:P].rearrange("p (b e) -> p b e", e=EXPERTS)
                total = bank[:, P:2 * P].rearrange("p (b e) -> p b e", e=EXPERTS)
                for e in range(EXPERTS):
                    ins = dve.tensor_tensor_scan(upto[:, :, e], ones[:, 0:BLOCKS], total[:, :, e], 0.0,
                                                 ALU.mult, ALU.add)
                chain(ins)
                chain(dve.tensor_tensor(place, within, upto, ALU.add))
                dve.tensor_tensor(place, place, total, ALU.subtract).then_inc(ring_sem["dve"], 1)
                wait_ring(dve, b, b.read(i), None)
                chain(dve.scalar_tensor_tensor(out=comb, in0=place, scalar=float(CAPACITY), in1=mask,
                                               op0=ALU.is_le, op1=ALU.mult))
                chain(dve.tensor_tensor(comb, comb, gates, ALU.mult))
                chain(dve.tensor_reduce(stats[:, 0, :], comb, AX.X, ALU.add))
                chain(dve.tensor_scalar(stats[:, 1, :], stats[:, 0, :], 1e-6, None, ALU.add))
                chain(dve.reciprocal(stats[:, 2, :], stats[:, 1, :]))
                dve.tensor_tensor(comb, comb, row(stats[:, 2, :]), ALU.mult).then_inc(comb_ready, 1)

            def weigh(t):
                dve.wait_ge(experts_done, t + 1)
                if t == 0:
                    dve.wait_ge(comb_ready, 1)
                if t >= 2:
                    dve.wait_ge(mixture_added, t - 1)
                dve.tensor_tensor(sums[:, t % 2, :].rearrange("p (e d) -> p e d", d=D),
                                  psum[t % 2][:, :].rearrange("p (e d) -> p e d", d=D),
                                  comb[:, t, :, None].to_broadcast([P, EXPERTS, D]), ALU.mult).then_inc(weighted, 1)

            def read(b, ev, k):
                if READER[ev[0]] != "dve":
                    return
                i = b.index(ev)
                bank = ring[b.bank(i)]
                kind = ev[0]
                if kind == "qk" and ev[2] == 0:
                    wait_pair(dve, low_done, b, CHUNKS, CHUNKS + ev[1], k)
                wait_ring(dve, b, b.full(i), k)
                if kind == "qk":
                    _, c, f = ev
                    blocks, own = slice(PER * c + 2 * f, PER * c + 2 * f + 2), slice(2 * f, 2 * f + 2)
                    raw = bank[:, :].rearrange("p (b g d) -> p b g d", g=4, d=DH)
                    t, u = t_rope[:, own], u_rope[:, own]
                    table = [P, 2, 4, DH // 2]
                    dve.tensor_tensor(t, raw, cos[:, blocks, None, :].to_broadcast([P, 2, 4, DH]), ALU.mult)
                    dve.tensor_tensor(u[:, :, :, 0:DH // 2], raw[:, :, :, 1:DH:2],
                                      sin[:, blocks, None, 0:DH // 2].to_broadcast(table), ALU.mult)
                    ins = dve.tensor_tensor(u[:, :, :, DH // 2:DH], raw[:, :, :, 0:DH:2],
                                            sin[:, blocks, None, DH // 2:DH].to_broadcast(table), ALU.mult)
                elif kind == "max":
                    _, h, i_, j = ev
                    ins = dve.tensor_reduce(mparts[:, BLOCKS * h + i_, j:j + 1], bank[:, :], AX.X, ALU.max)
                elif kind == "den":
                    ins = dve.transpose(o_norm, bank[:, :])
                elif kind == "proj":
                    c = ev[1]
                    part = acc[:, PER * c:PER * (c + 1), :]
                    ins = dve.tensor_tensor(part, bank[:, :].rearrange("p (b d) -> p b d", d=D), part, ALU.add)
                elif kind == "logit":
                    src = bank[:, 0:P].rearrange("p (b e) -> p b e", e=EXPERTS)
                    chain(dve.tensor_reduce(stats[:, 0, :], src, AX.X, ALU.max))
                    ins = dve.tensor_tensor(logits, src, row(stats[:, 0, :]), ALU.subtract)
                elif kind == "count":
                    keep(b, i, bank)
                    return
                ins.then_inc(ring_sem["dve"], 1)

            def invert(b, g, k):
                wait_ring(dve, b, b.read(b.index(("den", g % CHUNKS))), k)
                dve.reciprocal(inverse[:, :], o_norm[:, 0:CHUNK:BOX]).then_inc(inverted, 1)
                wait_pair(dve, inverted, b, 2 * CHUNKS, 2 * g + 1, k)
                dve.transpose(o_norm, inverse[:, :, None].to_broadcast([P, CHUNK // BOX, BOX])).then_inc(inverted, 1)

            def normalise(b, g, k):
                wait_pair(dve, o_copied, b, CHUNKS, g + 1, k)
                wait_pair(dve, inverted, b, 2 * CHUNKS, 2 * (g + 1), k)
                dve.tensor_tensor(o_norm, o_raw, o_norm, ALU.mult).then_inc(o_ready, 1)

            def low_parts(b, c, k):
                wait_pair(dve, high_done, b, CHUNKS, CHUNKS + c + 1, k)
                high = split[:, :, 0:8 * DH].rearrange("p g (a d) -> p g a d", d=DH)
                q_out = split_r[:, :, DH:3 * DH].rearrange("p g (a d) -> p g a d", d=DH)
                dve.tensor_tensor(q_out, t_rope[:, :, QA:KA, :], high[:, :, 0:4:3, :], ALU.subtract)
                k_out = split_r[:, :, 8 * DH:10 * DH].rearrange("p g (a d) -> p g a d", d=DH)
                dve.tensor_tensor(k_out, t_rope[:, :, KA:KB + 1, :], high[:, :, 4:8:2, :], ALU.subtract)\
                   .then_inc(low_done, 1)

            def add_exps(b, n, k):
                j = n % BLOCKS
                if j == 0:
                    return
                at = slice(SUM_POOL[n // BLOCKS], 2 * CHUNK)
                to = sums[:, (n // BLOCKS) % 2, at]
                wait_pair(dve, exp_done, b, STEPS, n + 1, k)
                if j > 1:
                    wait_pair(dve, summed_dve, b, CHUNKS * (BLOCKS - 1), sum_count(n - 1), k)
                dve.tensor_tensor(to, to if j > 1 else probs[:, (n - 1) % EXP_SLOTS, at],
                                  probs[:, n % EXP_SLOTS, at], ALU.add).then_inc(summed_dve, 1)

            def body(b, k=None):
                for n in range(STEPS):
                    for ev in b.steps[n]:
                        read(b, ev, k)
                    if b is first and n == 9:
                        choose()
                    if b is first and n - 1 in Y_AT:
                        weigh(Y_AT[n - 1])
                    if b.carry if n < BLOCKS else b.main:
                        if n % BLOCKS == INVERT_AT:
                            invert(b, n // BLOCKS - 1, k)
                        if n % BLOCKS == NORMALISE_AT:
                            normalise(b, n // BLOCKS - 1, k)
                    if b.prep and n == MAX_TO:
                        wait_ring(dve, b, b.read(max(i for i, ev in enumerate(b.order) if ev[0] == "max")), k)
                        dve.tensor_reduce(mneg[:, :], mparts[:, :, :], AX.X, ALU.max, negate=True)\
                           .then_inc(mneg_ready, 1)
                    if b is b0 and n == 1:
                        dve.wait_ge(mixture_added, BLOCKS)
                    if (b.main and n > 0) or (b.carry and n == 0):
                        add_exps(b, n - 1, k)
                    if b.prep and n % PREP_STRIDE == LOW_AT and n < PREP_STRIDE * CHUNKS:
                        low_parts(b, n // PREP_STRIDE, k)

            layernorm()
            dve.wait_ge(tables_here, 64)
            dve.wait_ge(consts_set, 1)
            body(pre)
            body(first)
            body(b0)
            with dve.Fori(0, ROUNDS) as k:
                body(odd, k)
                body(even, k)
            body(last)
            body(tail)

        @block.gpsimd
        def _(pool):
            chained = [0]

            def chain(ins):
                chained[0] += 1
                ins.then_inc(pool_chain, 1)
                pool.wait_ge(pool_chain, chained[0])

            def rope(b, c, k):
                wait_ring(pool, b, b.read(b.index(("qk", c, 1))), k)
                pool.tensor_tensor(t_rope, t_rope, u_rope, ALU.add).then_inc(roped, 1)
                wait_pair(pool, roped, b, 2 * CHUNKS, 2 * (CHUNKS + c) + 1, k)
                for g in range(PER):
                    ins = pool.tensor_tensor(t_rope[:, g], t_rope[:, g],
                                             fenc[:, PER * c + g, None, :].to_broadcast([P, 4, DH]), ALU.add)
                ins.then_inc(roped, 1)

            def add_up(t):
                pool.wait_ge(weighted, t + 1)
                z = sums[:, t % 2, :]
                for w in (4 * D, 2 * D, D):
                    chain(pool.tensor_tensor(z[:, 0:w], z[:, 0:w], z[:, w:2 * w], ALU.add))
                pool.tensor_tensor(acc[:, t, :], acc[:, t, :], z[:, 0:D], ALU.add).then_inc(mixture_added, 1)

            def add_exps(b, n, k):
                j = n % BLOCKS
                if j == 0:
                    return
                at = slice(0, SUM_POOL[n // BLOCKS])
                to = sums[:, (n // BLOCKS) % 2, at]
                wait_pair(pool, exp_done, b, STEPS, n + 1, k)
                if j == 1:
                    wait_pair(pool, o_ready, b, CHUNKS, n // BLOCKS - 1, k)
                else:
                    wait_pair(pool, summed_pool, b, CHUNKS * (BLOCKS - 1), sum_count(n - 1), k)
                pool.tensor_tensor(to, to if j > 1 else probs[:, (n - 1) % EXP_SLOTS, at],
                                   probs[:, n % EXP_SLOTS, at], ALU.add).then_inc(summed_pool, 1)

            def body(b, k=None):
                for n in range(STEPS):
                    if b.main:
                        add_exps(b, n, k)
                    if b.prep and n % PREP_STRIDE == ROPE_AT and n < PREP_STRIDE * CHUNKS:
                        rope(b, n // PREP_STRIDE, k)
                    if b is first and n - 2 in Y_AT:
                        add_up(Y_AT[n - 2])

            chain(pool.memset(ones[:, :], 1.0))
            for s in range(2):
                for h in range(2):
                    rows = (slice(DH, P), slice(0, DH))[h]
                    one = (slice(DH, DH + 1), slice(0, 1))[h]
                    chain(pool.memset(q2[s][h][rows, :].bitcast(F32), 0.0))
                    chain(pool.memset(k2[s][h][rows, :].bitcast(F32), 0.0))
                    chain(pool.memset(k2[s][h][one, :].bitcast(F32), 1.0))
            pool.sem_inc(consts_set, 1)
            pool.wait_ge(bo_here, 16)
            pool.wait_ge(var_ready, CHUNKS)
            chain(pool.tensor_tensor(acc[:, :, :], acc[:, :, :], bo[:, None, :].to_broadcast([P, BLOCKS, D]), ALU.add))
            wait_ring(pool, first, ("act", 0), None)
            body(first)
            body(b0)
            with pool.Fori(0, ROUNDS) as k:
                body(odd, k)
                body(even, k)
            body(last)


def kernel(L0_attn_x, L0_attn_w_qkv, L0_attn_w_fproj, L0_attn_b_fproj, L0_attn_w_out, L0_attn_b_out,
           L0_ffn_w_router, L0_ffn_w_gate, L0_ffn_w_down):
    import concourse.bacc as bacc
    from concourse.bass_utils import run_bass_kernel_spmd

    f = np.float32
    pos = np.arange(N, dtype=f)[:, None]
    freqs = f(10000.0) ** (-np.arange(0, DH, 2, dtype=f) / f(DH))
    angles = (pos * freqs.astype(f)).astype(f)
    sin = np.repeat(np.sin(angles), 2, axis=1).astype(f)
    cos = np.repeat(np.cos(angles), 2, axis=1).astype(f)
    sin[:, :DH // 2] *= -1
    four = pos * np.arange(1, FREQS + 1, dtype=f)
    fourier = np.concatenate([np.sin(four), np.cos(four), np.ones((N, 1), f)], 1).T.astype(f)

    def tokens(a):
        return np.ascontiguousarray(np.asarray(a).reshape(BLOCKS, P, -1).transpose(1, 0, 2))

    w_fproj = np.concatenate([np.asarray(L0_attn_w_fproj).T, np.asarray(L0_attn_b_fproj)[None]], 0)
    w_qkv = np.asarray(L0_attn_w_qkv).reshape(3, PAIRS, P, D).transpose(1, 3, 0, 2).reshape(PAIRS, D, 3 * P)
    arrays = {
        "x": tokens(L0_attn_x),
        "w_qkv": np.concatenate([w_qkv, w_qkv[:1]]),
        "w_fproj": w_fproj,
        "w_out": np.asarray(L0_attn_w_out).T.reshape(PAIRS, P, D),
        "b_out": np.asarray(L0_attn_b_out)[None],
        "w_router": np.asarray(L0_ffn_w_router).T,
        "w_gate": np.asarray(L0_ffn_w_gate).T,
        "w_down": np.asarray(L0_ffn_w_down).reshape(EXPERTS, D, 2, P).transpose(3, 2, 0, 1).reshape(P, 2, EXPERTS * D),
        "cos": tokens(cos),
        "sin": tokens(sin),
        "fourier": fourier,
        "ident": np.eye(P, dtype=f),
        "tri": np.triu(np.ones((P, P), f)),
        "lower": np.tril(np.ones((EXPERTS, EXPERTS), f), -1).reshape(1, -1),
    }
    nc = bacc.Bacc("TRN2", target_bir_lowering=False, num_devices=1)
    feeds, args = {}, []
    for name, a in arrays.items():
        a = np.ascontiguousarray(a)
        feeds[f"in_{name}"] = a
        args.append(nc.dram_tensor(f"in_{name}", a.shape, mybir.dt.from_np(a.dtype), kind="ExternalInput").ap())
    out = nc.dram_tensor("out", (P, BLOCKS, D), F32, kind="ExternalOutput").ap()
    attention_and_mixture(nc, *args, out)
    got = run_bass_kernel_spmd(nc, [feeds], core_ids=[0]).results[0]["out"]
    return np.asarray(got).transpose(1, 0, 2).reshape(1, N, D)
```

```python
from contextlib import ExitStack

import concourse.bass as bass
import numpy as np
from concourse import mybir

F32 = mybir.dt.float32
F32R = mybir.dt.float32r
ALU = mybir.AluOpType
ACT = mybir.ActivationFunctionType
AX = mybir.AxisListType

P = 128
N = 2048
D = 128
HEADS = 16
DH = 64
PAIRS = HEADS // 2
BLOCKS = N // P
CHUNK = 512
CHUNKS = N // CHUNK
PER = CHUNK // P
STEPS = CHUNKS * BLOCKS
FREQS = 16
HIDDEN = 256
EXPERTS = 8
TOP_K = 2
CAPACITY = -(-N * 5 // (EXPERTS * 4))
EPS = 1e-5
SCALE = DH ** -0.5

EXP_SLOTS = 4
SUM_POOL = (256, 512, 896, 896)
SUM_POOL_LAST = (448, 448, 448, 448)
WINDOWS = 5
WINDOW_ORDER = (2, 3, 0, 1, 4)
QA, QB, KA, KB = 0, 1, 2, 3

READER = {"qk": "dve", "max": "dve", "den": "dve", "proj": "dve", "logit": "dve", "count": "dve",
          "v": "act", "window": "act", "mt": "act", "hidden": "act", "xt": "act", "fenc": "act"}


PREP_STRIDE = 6
ROPE_AT, HIGH_AT, LOW_AT, VALUES_AT, WINDOWS_AT = 2, (4, 4, 5), 5, 6, 7
AHEAD = 3
MAX_FROM, MAX_TO = 11, 60
MT_STEP = 62
DEN_AT, INVERT_AT, NORMALISE_AT, PROJ_AT = 2, 3, 4, 8
BOX = 32
ADD_BIAS_AT, CHOOSE_AT, COUNT_AT, EXPERTS_AT, EXPERTS_TO = 12, 2, 7, 18, 61


def vector_load(n, main):
    load = 0
    if n < PREP_STRIDE * CHUNKS:
        load += 3 * (n % PREP_STRIDE < 2) + 2 * (n % PREP_STRIDE == LOW_AT)
    if main:
        load += 1.9 * (1 - SUM_POOL[n // BLOCKS] / (2 * CHUNK))
        load += n % BLOCKS in (DEN_AT, INVERT_AT, NORMALISE_AT, PROJ_AT)
    return load


def prep_events(steps, main):
    for c in range(CHUNKS):
        b = PREP_STRIDE * c
        ahead = AHEAD if c and not main else 0
        steps[b - ahead].append(("qk", c, 0))
        steps[b - ahead + 1].append(("qk", c, 1))
        steps[b + VALUES_AT].append(("v", c))
        for at, w in enumerate(WINDOW_ORDER):
            steps[b + WINDOWS_AT + at].append(("window", c, w))
    todo = [("max", h, i, j) for c in range(CHUNKS) for i in range(BLOCKS) for j in range(CHUNKS)
            for h in range(2) if max(i // PER, j) == c]
    load = [vector_load(n, main) for n in range(STEPS)]
    for n in range(MAX_FROM, MAX_TO + 1):
        share = (len(todo) + sum(load[n:MAX_TO + 1])) / (MAX_TO + 1 - n) - load[n]
        for _ in range(2 * round(share / 2)):
            if not todo:
                break
            chunk = max(todo[0][2] // PER, todo[0][3])
            if n < PREP_STRIDE * chunk + WINDOWS_AT + WINDOWS - 1:
                break
            steps[n].append(todo.pop(0))
    assert not todo
    steps[MT_STEP].append(("mt",))


class Body:

    def __init__(self, pair, main, carry, prep, extra=(), before=None, pair_stride=0):
        self.pair, self.main, self.carry, self.prep = pair, main, carry, prep
        self.pair_stride = pair_stride
        self.sum_pool = SUM_POOL if prep else SUM_POOL_LAST
        steps = [[] for _ in range(STEPS)]
        if carry:
            steps[DEN_AT].append(("den", CHUNKS - 1))
            steps[PROJ_AT].append(("proj", CHUNKS - 1))
        if prep:
            prep_events(steps, main)
        if main:
            for c in range(CHUNKS - 1):
                steps[BLOCKS * (c + 1) + DEN_AT].append(("den", c))
                steps[BLOCKS * (c + 1) + PROJ_AT].append(("proj", c))
        for n, ev in extra:
            steps[n].append(ev)
        for evs in steps:
            evs.sort(key=lambda ev: READER[ev[0]] != "act")
        self.steps = steps
        self.order = [ev for evs in steps for ev in evs]
        self.before = before
        self.count = {"full": len(self.order),
                      "dve": sum(READER[ev[0]] == "dve" for ev in self.order),
                      "act": sum(READER[ev[0]] == "act" for ev in self.order)}
        self.start = {s: before.start[s] + before.count[s] if before else 0 for s in self.count}
        self.stride = {s: 0 for s in self.count}

    def index(self, ev):
        return self.order.index(ev)

    def bank(self, i):
        return (i - len(self.order)) % 3

    def full(self, i):
        return "full", i + 1

    def read(self, i):
        r = READER[self.order[i][0]]
        return r, sum(READER[ev[0]] == r for ev in self.order[:i + 1])

    def last_user(self, i):
        if i >= 3:
            return self.read(i - 3)
        if self.before is None:
            return None
        bank = self.bank(i)
        back = (-bank) % 3 or 3
        tail = self.before.order[-back:]
        if len(tail) < back:
            return None
        r = READER[tail[0][0]]
        return r, -sum(READER[ev[0]] == r for ev in tail[1:])


def attention_and_mixture(nc, x_in, w_qkv, w_fproj, w_out, b_out, w_router, w_gate, w_down,
                          cos_in, sin_in, fourier, ident_in, tri_in, lower_in, out):
    with ExitStack() as ctx:
        def sb(name, shape, dt=F32):
            return ctx.enter_context(nc.sbuf_tensor(name, shape, dt))

        def sem(name):
            return ctx.enter_context(nc.semaphore(name))

        q1 = [[sb(f"q1_{s}{h}", [P, N], F32R) for h in range(2)] for s in range(2)]
        k1 = [[sb(f"k1_{s}{h}", [P, N], F32R) for h in range(2)] for s in range(2)]
        k2 = [[sb(f"k2_{s}{h}", [P, N], F32R) for h in range(2)] for s in range(2)]
        q2 = [[sb(f"q2_{s}{h}", [P, CHUNK], F32R) for h in range(2)] for s in range(2)]
        v = [sb(f"v_{s}", [P, BLOCKS, P]) for s in range(2)]
        xnT = sb("xnT", [P, N])
        acc = sb("acc", [P, BLOCKS, D])
        wp = [sb(f"wp_{s}", [P, 3 * P]) for s in range(2)]
        wo = [sb(f"wo_{s}", [P, D]) for s in range(2)]
        cos = sb("cos", [P, BLOCKS, DH])
        sin = sb("sin", [P, BLOCKS, DH])
        fenc = sb("fenc", [P, BLOCKS, DH])
        t_places = sb("t_places", [P, 2, PER, 4, DH])
        u_rope = sb("u_rope", [P, PER, 4, DH])
        split = sb("split", [P, PER, WINDOWS * P])
        probs = sb("probs", [P, EXP_SLOTS, 2 * CHUNK])
        sums = sb("sums", [P, 2, 2 * CHUNK])
        ob = sb("ob", [P, 2, CHUNK])
        mparts = sb("mparts", [P, 2 * BLOCKS, CHUNKS])
        mneg = sb("mneg", [P, 2 * BLOCKS])
        mrow = sb("mrow", [2 * BLOCKS, P], F32R)
        ident = sb("ident", [P, P])
        ident_r = sb("ident_r", [P, P], F32R)
        ones = sb("ones", [P, P])
        tri = sb("tri", [P, P])
        lower = sb("lower", [P, EXPERTS * EXPERTS])
        wf = sb("wf", [2 * FREQS + 1, DH])
        wr = sb("wr", [P, EXPERTS])
        wg = sb("wg", [P, HIDDEN])
        bo = sb("bo", [P, D])
        stats = sb("stats", [P, 5, BLOCKS])
        inverse = sb("inverse", [P, CHUNK // BOX])

        o_raw, o_norm = ob[:, 0, :], ob[:, 1, :]
        split_r = split[:, :, :].bitcast(F32R)
        hT = probs[:, :, :].rearrange("p a b -> p (a b)").rearrange("p (k n) -> p k n", k=2)
        wd = v[1][:, :, :].rearrange("p a b -> p (a b)").rearrange("p (k n) -> p k n", k=2)
        fourT = v[0][:, :, :].rearrange("p a b -> p (a b)")
        xc = sums[:, :, :].rearrange("p a b -> p (a b)").rearrange("p (b d) -> p b d", d=D)
        squares = t_places[:, :, :, :, :].rearrange("p a b c d -> p (a b c d)")
        beats = sums[:, 0, :].rearrange("p (b e f) -> p b e f", e=EXPERTS, f=EXPERTS)
        ties = sums[:, 1, :].rearrange("p (b e f) -> p b e f", e=EXPERTS, f=EXPERTS)
        small = ob[:, :, :].rearrange("p a (s b e) -> p (a s) b e", s=4, e=EXPERTS)
        logits, gates, rank, mask, upto, place, comb = (small[:, i] for i in range(7))

        psum = [ctx.enter_context(nc.psum_tensor(f"scores_{i}", [P, 2 * CHUNK], F32)) for i in range(2)]
        ring = [ctx.enter_context(nc.psum_tensor(f"ring_{i}", [P, CHUNK], F32)) for i in range(3)]
        oT = ctx.enter_context(nc.psum_tensor("oT", [P, CHUNK], F32))

        x_here = [sem(f"x_here{c}") for c in range(CHUNKS)]
        ident_here, tables_here, four_here = sem("ident_here"), sem("tables_here"), sem("four_here")
        router_here, gate_here, down_here = sem("router_here"), sem("gate_here"), sem("down_here")
        bo_here, tri_here, lower_here = sem("bo_here"), sem("tri_here"), sem("lower_here")
        wp_here = [sem(f"wp_here{s}") for s in range(2)]
        wo_here = [sem(f"wo_here{s}") for s in range(2)]
        q2_here = [sem(f"q2_here{s}") for s in range(2)]
        out_there = sem("out_there")
        consts_set = sem("consts_set")
        dve_chain = sem("dve_chain")
        centred, squared, root_taken, xn_ready = sem("centred"), sem("squared"), sem("root_taken"), sem("xn_ready")
        var_ready = sem("var_ready")
        exped_gates, mask_ready, comb_ready = sem("exped_gates"), sem("mask_ready"), sem("comb_ready")
        experts_done, weighted, mixture_added = sem("experts_done"), sem("weighted"), sem("mixture_added")
        pool_chain = sem("pool_chain")
        ring_sem = {"full": sem("ring_full"), "dve": sem("ring_read_dve"), "act": sem("ring_read_act")}
        roped, high_done, low_done, mneg_ready = sem("roped"), sem("high_done"), sem("low_done"), sem("mneg_ready")
        scores_done, exp_done, values_done = sem("scores_done"), sem("exp_done"), sem("values_done")
        summed_dve, summed_pool = sem("summed_dve"), sem("summed_pool")
        o_copied, inverted, o_ready = sem("o_copied"), sem("inverted"), sem("o_ready")

        pre = Body(-1, False, False, False,
                   extra=[(0, ("fenc", 0)), (1, ("fenc", 1))] + [(2 + c, ("xt", c)) for c in range(CHUNKS)])
        first = Body(-1, False, False, True, before=pre, extra=
                     [(1, ("logit",))] + [(2 + i // 2, ("hidden", i % 2, i // 2)) for i in range(8)]
                     + [(COUNT_AT, ("count",))])
        products = 4 * BLOCKS
        PRODUCT_AT = [3 * EXPERTS_AT + 3 * (EXPERTS_TO - EXPERTS_AT) * i // products for i in range(products)]
        WEIGH_AT = {PRODUCT_AT[4 * b + 3] // 3 + 1: b for b in range(BLOCKS)}
        b0 = Body(0, True, False, True, before=first)
        odd = Body(1, True, True, True, before=b0, pair_stride=2)
        even = Body(2, True, True, True, before=odd, pair_stride=2)
        ROUNDS = (PAIRS - 2) // 2
        for b in (odd, even):
            b.stride = {s: odd.count[s] + even.count[s] for s in b.count}
        last = Body(PAIRS - 1, True, True, False, before=even)
        last.start = {s: odd.start[s] + ROUNDS * odd.stride[s] for s in odd.start}
        tail = Body(PAIRS, False, True, False, before=last)

        def t_place(b, c):
            return t_places[:, 1 if b is first and c % 2 else 0]

        def pair_count(b, per, local, k):
            base = per * b.pair + local
            return base if k is None or not b.pair_stride else k * (per * b.pair_stride) + base

        def wait_pair(eng, s, b, per, local, k):
            if k is not None or per * b.pair + local > 0:
                eng.wait_ge(s, pair_count(b, per, local, k))

        def wait_ring(eng, b, what, k):
            if what is None:
                return
            s, local = what
            base = b.start[s] + local
            if k is not None or base > 0:
                eng.wait_ge(ring_sem[s], base if k is None else k * b.stride[s] + base)

        def sum_count(n):
            return (BLOCKS - 1) * (n // BLOCKS) + max(n % BLOCKS, 1)

        block = ctx.enter_context(nc.Block())

        @block.sync
        def _(sp):
            def load(dst, src, s):
                sp.dma_start(dst, src).then_inc(s, 16)

            def pair_loads(b, k):
                s = b.pair % 2
                pair = b.pair + (0 if k is None else k * b.pair_stride)
                if b.main:
                    wait_pair(sp, scores_done, b, STEPS, 0, k)
                    query_chunk(s, 1)
                    if b.prep:
                        load(wp[s][:, :], w_qkv[pair + 2], wp_here[s])
                    wait_pair(sp, scores_done, b, STEPS, BLOCKS + 1, k)
                    query_chunk(s, 2)
                    if b.prep:
                        load(wo[1 - s][:, :], w_out[pair + 1], wo_here[1 - s])
                    wait_pair(sp, scores_done, b, STEPS, 2 * BLOCKS, k)
                    query_chunk(s, 3)
                if b.prep:
                    if b.main:
                        wait_pair(sp, scores_done, b, STEPS, 3 * BLOCKS, k)
                    else:
                        wait_ring(sp, b, b.read(b.index(("window", 0, 1))), k)
                    query_rows(1 - s, 0)
                    wait_ring(sp, b, b.read(b.index(("mt",))), k)
                    maximum_rows(0)

            def query_rows(s, c):
                at = slice(c * CHUNK, (c + 1) * CHUNK)
                for h, rows in ((0, slice(0, DH)), (1, slice(DH, P))):
                    load(q2[c % 2][h][rows, :].bitcast(F32), q1[s][h][rows, at].bitcast(F32), q2_here[c % 2])

            def maximum_rows(c):
                for h, row in ((0, slice(DH, DH + 1)), (1, slice(0, 1))):
                    first_block = BLOCKS * h + PER * c
                    load(q2[c % 2][h][row, :].bitcast(F32), mrow[first_block:first_block + PER, :].bitcast(F32),
                         q2_here[c % 2])

            def query_chunk(s, c):
                query_rows(s, c)
                maximum_rows(c)

            for c in range(CHUNKS):
                load(acc[:, PER * c:PER * (c + 1), :], x_in[:, PER * c:PER * (c + 1), :], x_here[c])
            load(fourT[0:2 * FREQS + 1, :], fourier, four_here)
            load(wf[:, :], w_fproj, four_here)
            load(ident[:, :], ident_in, ident_here)
            load(wp[0][:, :], w_qkv[0], wp_here[0])
            load(cos[:, :, :], cos_in, tables_here)
            load(sin[:, :, :], sin_in, tables_here)
            load(wr[:, :], w_router, router_here)
            load(lower[:, :], lower_in.to_broadcast([P, EXPERTS * EXPERTS]), lower_here)
            load(wg[:, :], w_gate, gate_here)
            load(tri[:, :], tri_in, tri_here)
            load(bo[:, :], b_out.to_broadcast([P, D]), bo_here)
            load(wd, w_down, down_here)
            load(wp[1][:, :], w_qkv[1], wp_here[1])
            load(wo[0][:, :], w_out[0], wo_here[0])
            sp.wait_ge(consts_set, 1)
            pair_loads(first, None)
            pair_loads(b0, None)
            with sp.Fori(0, ROUNDS) as k:
                pair_loads(odd, k)
                pair_loads(even, k)
            pair_loads(last, None)
            for c in range(CHUNKS):
                b = last if c < CHUNKS - 1 else tail
                wait_ring(sp, b, b.read(b.index(("proj", c))), None)
                load(out[:, PER * c:PER * (c + 1), :], acc[:, PER * c:PER * (c + 1), :], out_there)
            sp.wait_ge(out_there, 16 * CHUNKS)

        @block.tensor
        def _(pe):
            def mm(o, l, r, start=True, stop=True, **more):
                return pe.matmul(o, l, r, start=start, stop=stop, skip_group_check=True, **more)

            def scores(b, n, h, k):
                c, j, s = n // BLOCKS, n % BLOCKS, b.pair % 2
                if n == 0 and h == 0:
                    wait_ring(pe, b, ("act", 0), k)
                    if b.pair == 0:
                        pe.wait_ge(weighted, BLOCKS)
                if j == 0 and h == 0:
                    wait_pair(pe, q2_here[c % 2], b, 128, 64 * (c // 2 + 1), k)
                if h == 0:
                    wait_pair(pe, exp_done, b, STEPS, n - 1, k)
                keys, queries = slice(P * j, P * (j + 1)), slice(CHUNK * c, CHUNK * (c + 1))
                o = psum[n % 2][:, CHUNK * h:CHUNK * (h + 1)]
                mm(o, k1[s][h][:, keys], q1[s][h][:, queries], stop=False)
                last_mm = mm(o, k2[s][h][:, keys], q2[c % 2][h][:, :], start=False)
                if h == 1:
                    last_mm.then_inc(scores_done, 1)

            def values(b, n, k):
                j, s = n % BLOCKS, (b.pair + (n < 0)) % 2
                wait_pair(pe, exp_done, b, STEPS, n + 1, k)
                if j == 0:
                    wait_pair(pe, o_copied, b, CHUNKS, n // BLOCKS, k)
                for h in range(2):
                    last_mm = mm(oT[DH * h:DH * (h + 1), :], v[s][:, j, DH * h:DH * (h + 1)],
                                 probs[:, n % EXP_SLOTS, CHUNK * h:CHUNK * (h + 1)],
                                 start=(j == 0), stop=(j == BLOCKS - 1))
                last_mm.then_inc(values_done, 1)

            def fill(b, ev, seen, k):
                i = b.index(ev)
                bank = ring[b.bank(i)]
                wait_ring(pe, b, b.last_user(i), k)
                kind = ev[0]
                s = (b.pair + 1) % 2
                if kind == "qk":
                    _, c, f = ev
                    if c == 0 and f == 0:
                        wait_pair(pe, wp_here[s], b, 8, 24 if s == 0 else 16, k)
                    for g in range(2):
                        t = PER * c + 2 * f + g
                        last_mm = mm(bank[:, 2 * P * g:2 * P * (g + 1)], xnT[:, P * t:P * (t + 1)],
                                     wp[s][:, 0:2 * P])
                elif kind == "v":
                    for g in range(PER):
                        t = PER * ev[1] + g
                        last_mm = mm(bank[:, P * g:P * (g + 1)], xnT[:, P * t:P * (t + 1)], wp[s][:, 2 * P:3 * P])
                elif kind == "window":
                    _, c, w = ev
                    if w == WINDOW_ORDER[0]:
                        wait_pair(pe, high_done, b, CHUNKS, CHUNKS + c + 1, k)
                    if w == 0:
                        wait_pair(pe, low_done, b, CHUNKS, CHUNKS + c + 1, k)
                    for g in range(PER):
                        last_mm = pe.transpose(bank[:, P * g:P * (g + 1)].bitcast(F32R),
                                               split_r[:, g, P * w:P * (w + 1)], ident_r[:, :])
                elif kind == "max":
                    _, h, i_, j = ev
                    need = b.read(b.index(("window", max(i_ // PER, j), 1)))
                    if need not in seen:
                        wait_ring(pe, b, need, k)
                        seen.append(need)
                    rows = slice(DH * h, DH * (h + 1))
                    last_mm = mm(bank[:, :], q1[s][h][rows, P * i_:P * (i_ + 1)],
                                 k1[s][h][rows, CHUNK * j:CHUNK * (j + 1)])
                elif kind == "mt":
                    wait_pair(pe, mneg_ready, b, 1, 2, k)
                    last_mm = pe.transpose(bank[0:2 * BLOCKS, 0:P], mneg[:, :], ident[:, :])
                elif kind == "den":
                    g = ev[1] + (-CHUNKS if b.carry and ev[1] == CHUNKS - 1 else 0)
                    for q in (summed_dve, summed_pool):
                        wait_pair(pe, q, b, CHUNKS * (BLOCKS - 1), (BLOCKS - 1) * (g + 1), k)
                    for h in range(2):
                        last_mm = mm(bank[DH * h:DH * (h + 1), :], ones[:, 0:DH],
                                     sums[:, ev[1] % 2, CHUNK * h:CHUNK * (h + 1)])
                elif kind == "proj":
                    g = ev[1] + (-CHUNKS if b.carry and ev[1] == CHUNKS - 1 else 0)
                    s = (b.pair + (g < 0)) % 2
                    if ev[1] == 0 and b.main:
                        wait_pair(pe, wo_here[s], b, 8, 16 if s == 0 else 8, k)
                    wait_pair(pe, o_ready, b, CHUNKS, g + 1, k)
                    for t in range(PER):
                        last_mm = mm(bank[:, P * t:P * (t + 1)], o_norm[:, P * t:P * (t + 1)], wo[s][:, :])
                elif kind == "xt":
                    pe.wait_ge(xn_ready, ev[1] + 1)
                    if ev[1] == 0:
                        pe.wait_ge(ident_here, 16)
                    for g in range(PER):
                        last_mm = pe.transpose(bank[:, P * g:P * (g + 1)], xc[:, PER * ev[1] + g, :], ident[:, :])
                elif kind == "fenc":
                    pe.wait_ge(four_here, 32)
                    for g in range(8):
                        t = 8 * ev[1] + g
                        last_mm = mm(bank[:, DH * g:DH * (g + 1)], fourT[0:2 * FREQS + 1, P * t:P * (t + 1)], wf[:, :])
                elif kind == "logit":
                    pe.wait_ge(router_here, 16)
                    for t in range(BLOCKS):
                        last_mm = mm(bank[:, EXPERTS * t:EXPERTS * (t + 1)], xnT[:, P * t:P * (t + 1)], wr[:, :])
                elif kind == "hidden":
                    pe.wait_ge(gate_here, 16)
                    last_mm = mm(bank[:, :], wg[:, P * ev[1]:P * (ev[1] + 1)], xnT[:, CHUNK * ev[2]:CHUNK * (ev[2] + 1)])
                elif kind == "count":
                    pe.wait_ge(mask_ready, 1)
                    pe.wait_ge(tri_here, 16)
                    pe.wait_ge(consts_set, 1)
                    flat = mask.rearrange("p b e -> p (b e)")
                    mm(bank[:, 0:P], tri[:, :], flat)
                    last_mm = mm(bank[:, P:2 * P], ones[:, :], flat)
                last_mm.then_inc(ring_sem["full"], 1)

            def experts(b, i):
                t, half, q = i // 4, i // 2 % 2, i % 2
                if i == 0:
                    pe.wait_ge(down_here, 16)
                    wait_ring(pe, b, b.read(b.index(("hidden", 1, CHUNKS - 1))), None)
                if t >= 2 and i % 4 == 0:
                    pe.wait_ge(weighted, t - 1)
                last_mm = mm(psum[t % 2][:, CHUNK * half:CHUNK * (half + 1)], hT[:, q, P * t:P * (t + 1)],
                             wd[:, q, CHUNK * half:CHUNK * (half + 1)], start=(q == 0), stop=(q == 1))
                if i % 4 == 3:
                    last_mm.then_inc(experts_done, 1)

            def body(b, k=None):
                seen = []
                for n in range(STEPS):
                    mine = [ev for ev in b.steps[n] if READER[ev[0]] == "act"]
                    rest = [ev for ev in b.steps[n] if READER[ev[0]] != "act"]
                    cuts = ((0, 0, 0), (0, 1, 0), (0, 2, 0), (1, 0, 2), (0, 2, 2), (1, 2, 2), (2, 2, 2))[len(rest)]
                    for ev in mine:
                        fill(b, ev, seen, k)
                    for part in range(3):
                        if b.main and part < 2:
                            scores(b, n, part, k)
                        if part == 2 and ((b.main and n > 0) or (b.carry and n == 0)):
                            values(b, n - 1, k)
                        for ev in rest[sum(cuts[:part]):sum(cuts[:part + 1])]:
                            fill(b, ev, seen, k)
                        for i in range(4 * BLOCKS):
                            if b is first and PRODUCT_AT[i] == 3 * n + part:
                                experts(b, i)

            body(pre)
            wait_ring(pe, first, ("act", 0), None)
            body(first)
            body(b0)
            with pe.Fori(0, ROUNDS) as k:
                body(odd, k)
                body(even, k)
            body(last)
            body(tail)

        @block.scalar
        def _(act):
            def read(b, ev, k):
                if READER[ev[0]] != "act":
                    return
                i = b.index(ev)
                bank = ring[b.bank(i)]
                s = (b.pair + 1) % 2
                kind = ev[0]
                if kind == "v" and ev[1] == 0:
                    wait_pair(act, values_done, b, STEPS, 0, k)
                wait_ring(act, b, b.full(i), k)
                if kind == "v":
                    c = ev[1]
                    ins = act.copy(v[s][:, PER * c:PER * (c + 1), :], bank[:, :])
                elif kind == "window":
                    _, c, w = ev
                    at = slice(CHUNK * c, CHUNK * (c + 1))
                    if w < 4:
                        ins = act.copy((q1, q1, k1, k1)[w][s][w % 2][:, at], bank[:, :])
                    else:
                        act.copy(k2[s][0][0:DH, at], bank[0:DH, :])
                        ins = act.copy(k2[s][1][DH:P, at], bank[DH:P, :])
                elif kind == "mt":
                    ins = act.copy(mrow[:, :], bank[0:2 * BLOCKS, 0:P])
                elif kind == "xt":
                    ins = act.copy(xnT[:, CHUNK * ev[1]:CHUNK * (ev[1] + 1)], bank[:, :])
                elif kind == "fenc":
                    ins = act.copy(fenc[:, 8 * ev[1]:8 * (ev[1] + 1), :], bank[:, :])
                elif kind == "hidden":
                    ins = act.activation(hT[:, ev[1], CHUNK * ev[2]:CHUNK * (ev[2] + 1)], bank[:, :], ACT.Silu)
                ins.then_inc(ring_sem["act"], 1)

            def weigh(t):
                act.wait_ge(experts_done, t + 1)
                if t == 0:
                    act.wait_ge(comb_ready, 1)
                if t >= 2:
                    act.wait_ge(mixture_added, t - 1)
                for e in range(EXPERTS):
                    at = slice(D * e, D * (e + 1))
                    ins = act.mul(sums[:, t % 2, at], psum[t % 2][:, at], comb[:, t, e:e + 1])
                ins.then_inc(weighted, 1)

            def exps(b, n, k):
                wait_pair(act, scores_done, b, STEPS, n + 1, k)
                wait_pair(act, values_done, b, STEPS, n - EXP_SLOTS + 1, k)
                for q in (summed_dve, summed_pool):
                    wait_pair(act, q, b, CHUNKS * (BLOCKS - 1), sum_count(n - EXP_SLOTS), k)
                act.activation(probs[:, n % EXP_SLOTS, :], psum[n % 2][:, :], ACT.Exp, scale=SCALE)\
                   .then_inc(exp_done, 1)

            def copy_output(b, g, k):
                wait_pair(act, values_done, b, STEPS, BLOCKS * (g + 1), k)
                wait_pair(act, o_ready, b, CHUNKS, g, k)
                act.copy(o_raw, oT[:, :]).then_inc(o_copied, 1)

            def high_parts(b, c, piece, k):
                t_rope = t_place(b, c)
                if piece == 0:
                    wait_pair(act, roped, b, 2 * CHUNKS, 2 * (CHUNKS + c + 1), k)
                    q_out = split_r[:, :, 0:4 * DH].rearrange("p g (a d) -> p g a d", d=DH)[:, :, 0:4:3, :]
                    act.copy(q_out, t_rope[:, :, QA:KA, :])
                    return
                k_out = split_r[:, :, 4 * DH:8 * DH].rearrange("p g (a t d) -> p g a t d", t=2, d=DH)
                ins = act.copy(k_out[:, :, :, piece - 1, :], t_rope[:, :, KA:KB + 1, :])
                if piece == 2:
                    ins.then_inc(high_done, 1)

            def body(b, k=None):
                for n in range(STEPS):
                    if b is first and n in WEIGH_AT:
                        weigh(WEIGH_AT[n])
                    if b is first and n == 2:
                        wait_ring(act, b, b.read(b.index(("logit",))), k)
                        act.activation(gates, logits, ACT.Exp).then_inc(exped_gates, 1)
                    for ev in b.steps[n]:
                        read(b, ev, k)
                    if b.main:
                        exps(b, n, k)
                    if b.main and n % BLOCKS == 0 and n:
                        copy_output(b, n // BLOCKS - 1, k)
                    if b.carry and n == 0:
                        copy_output(b, -1, k)
                    for piece, at in enumerate(HIGH_AT):
                        if b.prep and n % PREP_STRIDE == at and n < PREP_STRIDE * CHUNKS:
                            high_parts(b, n // PREP_STRIDE, piece, k)

            for c in range(CHUNKS):
                act.wait_ge(centred, c + 1)
                act.activation(squares[:, CHUNK * c:CHUNK * (c + 1)], xc[:, PER * c:PER * (c + 1), :], ACT.Square)\
                   .then_inc(squared, 1)
            for c in range(CHUNKS):
                act.wait_ge(var_ready, c + 1)
                act.activation(stats[:, 3, PER * c:PER * (c + 1)], stats[:, 2, PER * c:PER * (c + 1)], ACT.Sqrt)\
                   .then_inc(root_taken, 1)
            act.wait_ge(ident_here, 16)
            act.copy(ident_r[:, :], ident[:, :])
            body(pre)
            body(first)
            body(b0)
            with act.Fori(0, ROUNDS) as k:
                body(odd, k)
                body(even, k)
            body(last)
            body(tail)

        @block.vector
        def _(dve):
            chained = [0]

            def chain(ins):
                chained[0] += 1
                ins.then_inc(dve_chain, 1)
                dve.wait_ge(dve_chain, chained[0])

            def layernorm():
                for c in range(CHUNKS):
                    x, y = acc[:, PER * c:PER * (c + 1), :], xc[:, PER * c:PER * (c + 1), :]
                    st = [stats[:, i, PER * c:PER * (c + 1)] for i in range(5)]
                    dve.wait_ge(x_here[c], 16)
                    chain(dve.tensor_reduce(st[0], x, AX.X, ALU.add))
                    chain(dve.tensor_scalar(st[1], st[0], -1.0 / D, None, ALU.mult))
                    dve.tensor_tensor(y, x, st[1][:, :, None].to_broadcast([P, PER, D]), ALU.add)\
                       .then_inc(centred, 1)
                for c in range(CHUNKS):
                    st = [stats[:, i, PER * c:PER * (c + 1)] for i in range(5)]
                    dve.wait_ge(squared, c + 1)
                    chain(dve.tensor_reduce(st[0], squares[:, CHUNK * c:CHUNK * (c + 1)].rearrange(
                        "p (b d) -> p b d", d=D), AX.X, ALU.add))
                    dve.tensor_scalar(st[2], st[0], 1.0 / D, EPS, ALU.mult, ALU.add).then_inc(var_ready, 1)
                for c in range(CHUNKS):
                    y = xc[:, PER * c:PER * (c + 1), :]
                    st = [stats[:, i, PER * c:PER * (c + 1)] for i in range(5)]
                    dve.wait_ge(root_taken, c + 1)
                    chain(dve.reciprocal(st[4], st[3]))
                    dve.tensor_tensor(y, y, st[4][:, :, None].to_broadcast([P, PER, D]), ALU.mult).then_inc(xn_ready, 1)

            def wide(t, axis):
                t = t[:, :, None, :] if axis == 2 else t[:, :, :, None]
                return t.to_broadcast([P, BLOCKS, EXPERTS, EXPERTS])

            def row(t):
                return t[:, :, None].to_broadcast([P, BLOCKS, EXPERTS])

            def choose():
                dve.wait_ge(exped_gates, 1)
                dve.wait_ge(lower_here, 16)
                chain(dve.tensor_reduce(stats[:, 0, :], gates, AX.X, ALU.add))
                chain(dve.reciprocal(stats[:, 1, :], stats[:, 0, :]))
                chain(dve.tensor_tensor(gates, gates, row(stats[:, 1, :]), ALU.mult))
                dve.tensor_tensor(beats, wide(gates, 2), wide(gates, 3), ALU.is_gt)
                chain(dve.tensor_tensor(ties, wide(gates, 2), wide(gates, 3), ALU.is_equal))
                flat_ties = ties.rearrange("p b e f -> p b (e f)")
                chain(dve.tensor_tensor(flat_ties, flat_ties, lower[:, None, :].to_broadcast(
                    [P, BLOCKS, EXPERTS * EXPERTS]), ALU.mult))
                chain(dve.tensor_tensor(beats, beats, ties, ALU.add))
                chain(dve.tensor_reduce(rank, beats, AX.X, ALU.add))
                dve.tensor_scalar(mask, rank, float(TOP_K), None, ALU.is_lt).then_inc(mask_ready, 1)

            def keep(b, i, bank):
                within = bank[:, 0:P].rearrange("p (b e) -> p b e", e=EXPERTS)
                total = bank[:, P:2 * P].rearrange("p (b e) -> p b e", e=EXPERTS)
                for e in range(EXPERTS):
                    ins = dve.tensor_tensor_scan(upto[:, :, e], ones[:, 0:BLOCKS], total[:, :, e], 0.0,
                                                 ALU.mult, ALU.add)
                chain(ins)
                chain(dve.tensor_tensor(place, within, upto, ALU.add))
                dve.tensor_tensor(place, place, total, ALU.subtract).then_inc(ring_sem["dve"], 1)
                wait_ring(dve, b, b.read(i), None)
                chain(dve.scalar_tensor_tensor(out=comb, in0=place, scalar=float(CAPACITY), in1=mask,
                                               op0=ALU.is_le, op1=ALU.mult))
                chain(dve.tensor_tensor(comb, comb, gates, ALU.mult))
                chain(dve.tensor_reduce(stats[:, 0, :], comb, AX.X, ALU.add))
                chain(dve.tensor_scalar(stats[:, 1, :], stats[:, 0, :], 1e-6, None, ALU.add))
                chain(dve.reciprocal(stats[:, 2, :], stats[:, 1, :]))
                dve.tensor_tensor(comb, comb, row(stats[:, 2, :]), ALU.mult).then_inc(comb_ready, 1)

            def read(b, ev, k):
                if READER[ev[0]] != "dve":
                    return
                i = b.index(ev)
                bank = ring[b.bank(i)]
                kind = ev[0]
                if kind == "qk" and ev[2] == 0:
                    wait_pair(dve, low_done, b, CHUNKS, CHUNKS + ev[1] - (b is first), k)
                    if b is first:
                        wait_pair(dve, roped, b, 2 * CHUNKS, 2 * (CHUNKS + ev[1]) - 1, k)
                wait_ring(dve, b, b.full(i), k)
                if kind == "qk":
                    _, c, f = ev
                    blocks, own = slice(PER * c + 2 * f, PER * c + 2 * f + 2), slice(2 * f, 2 * f + 2)
                    raw = bank[:, :].rearrange("p (b g d) -> p b g d", g=4, d=DH)
                    t, u = t_place(b, c)[:, own], u_rope[:, own]
                    table = [P, 2, 4, DH // 2]
                    dve.tensor_tensor(t, raw, cos[:, blocks, None, :].to_broadcast([P, 2, 4, DH]), ALU.mult)
                    dve.tensor_tensor(u[:, :, :, 0:DH // 2], raw[:, :, :, 1:DH:2],
                                      sin[:, blocks, None, 0:DH // 2].to_broadcast(table), ALU.mult)
                    ins = dve.tensor_tensor(u[:, :, :, DH // 2:DH], raw[:, :, :, 0:DH:2],
                                            sin[:, blocks, None, DH // 2:DH].to_broadcast(table), ALU.mult)
                elif kind == "max":
                    _, h, i_, j = ev
                    ins = dve.tensor_reduce(mparts[:, BLOCKS * h + i_, j:j + 1], bank[:, :], AX.X, ALU.max)
                elif kind == "den":
                    ins = dve.transpose(o_norm, bank[:, :])
                elif kind == "proj":
                    c = ev[1]
                    part = acc[:, PER * c:PER * (c + 1), :]
                    ins = dve.tensor_tensor(part, bank[:, :].rearrange("p (b d) -> p b d", d=D), part, ALU.add)
                elif kind == "logit":
                    src = bank[:, 0:P].rearrange("p (b e) -> p b e", e=EXPERTS)
                    chain(dve.tensor_reduce(stats[:, 0, :], src, AX.X, ALU.max))
                    ins = dve.tensor_tensor(logits, src, row(stats[:, 0, :]), ALU.subtract)
                elif kind == "count":
                    keep(b, i, bank)
                    return
                ins.then_inc(ring_sem["dve"], 1)

            def invert(b, g, k):
                wait_ring(dve, b, b.read(b.index(("den", g % CHUNKS))), k)
                dve.reciprocal(inverse[:, :], o_norm[:, 0:CHUNK:BOX]).then_inc(inverted, 1)
                wait_pair(dve, inverted, b, 2 * CHUNKS, 2 * g + 1, k)
                dve.transpose(o_norm, inverse[:, :, None].to_broadcast([P, CHUNK // BOX, BOX])).then_inc(inverted, 1)

            def normalise(b, g, k):
                wait_pair(dve, o_copied, b, CHUNKS, g + 1, k)
                wait_pair(dve, inverted, b, 2 * CHUNKS, 2 * (g + 1), k)
                dve.tensor_tensor(o_norm, o_raw, o_norm, ALU.mult).then_inc(o_ready, 1)

            def low_parts(b, c, k):
                wait_pair(dve, high_done, b, CHUNKS, CHUNKS + c + 1, k)
                high = split[:, :, 0:8 * DH].rearrange("p g (a d) -> p g a d", d=DH)
                q_out = split_r[:, :, DH:3 * DH].rearrange("p g (a d) -> p g a d", d=DH)
                t_rope = t_place(b, c)
                dve.tensor_tensor(q_out, t_rope[:, :, QA:KA, :], high[:, :, 0:4:3, :], ALU.subtract)
                k_out = split_r[:, :, 8 * DH:10 * DH].rearrange("p g (a d) -> p g a d", d=DH)
                dve.tensor_tensor(k_out, t_rope[:, :, KA:KB + 1, :], high[:, :, 4:8:2, :], ALU.subtract)\
                   .then_inc(low_done, 1)

            def add_exps(b, n, k):
                j = n % BLOCKS
                if j == 0:
                    return
                owner = b if n >= 0 else b.before
                at = slice(owner.sum_pool[n // BLOCKS], 2 * CHUNK)
                to = sums[:, (n // BLOCKS) % 2, at]
                wait_pair(dve, exp_done, b, STEPS, n + 1, k)
                if j > 1:
                    wait_pair(dve, summed_dve, b, CHUNKS * (BLOCKS - 1), sum_count(n - 1), k)
                dve.tensor_tensor(to, to if j > 1 else probs[:, (n - 1) % EXP_SLOTS, at],
                                  probs[:, n % EXP_SLOTS, at], ALU.add).then_inc(summed_dve, 1)

            def body(b, k=None):
                for n in range(STEPS):
                    for ev in b.steps[n]:
                        read(b, ev, k)
                    if b is first and n == CHOOSE_AT:
                        choose()
                    if b.carry if n < BLOCKS else b.main:
                        if n % BLOCKS == INVERT_AT:
                            invert(b, n // BLOCKS - 1, k)
                        if n % BLOCKS == NORMALISE_AT:
                            normalise(b, n // BLOCKS - 1, k)
                    if b.prep and n == MAX_TO:
                        wait_ring(dve, b, b.read(max(i for i, ev in enumerate(b.order) if ev[0] == "max")), k)
                        dve.tensor_reduce(mneg[:, :], mparts[:, :, :], AX.X, ALU.max, negate=True)\
                           .then_inc(mneg_ready, 1)
                    if b is b0 and n == 1:
                        dve.wait_ge(mixture_added, BLOCKS)
                    if (b.main and n > 0) or (b.carry and n == 0):
                        add_exps(b, n - 1, k)
                    if b.prep and n % PREP_STRIDE == LOW_AT and n < PREP_STRIDE * CHUNKS:
                        low_parts(b, n // PREP_STRIDE, k)

            layernorm()
            dve.wait_ge(tables_here, 32)
            dve.wait_ge(consts_set, 1)
            body(pre)
            body(first)
            body(b0)
            with dve.Fori(0, ROUNDS) as k:
                body(odd, k)
                body(even, k)
            body(last)
            body(tail)

        @block.gpsimd
        def _(pool):
            chained = [0]

            def chain(ins):
                chained[0] += 1
                ins.then_inc(pool_chain, 1)
                pool.wait_ge(pool_chain, chained[0])

            def rope(b, c, k):
                wait_ring(pool, b, b.read(b.index(("qk", c, 1))), k)
                t_rope = t_place(b, c)
                pool.tensor_tensor(t_rope, t_rope, u_rope[:, :, :, :], ALU.add).then_inc(roped, 1)
                wait_pair(pool, roped, b, 2 * CHUNKS, 2 * (CHUNKS + c) + 1, k)
                for g in range(PER):
                    ins = pool.tensor_tensor(t_rope[:, g], t_rope[:, g],
                                             fenc[:, PER * c + g, None, :].to_broadcast([P, 4, DH]), ALU.add)
                ins.then_inc(roped, 1)

            def add_up(t):
                pool.wait_ge(weighted, t + 1)
                z = sums[:, t % 2, :]
                for w in (4 * D, 2 * D, D):
                    chain(pool.tensor_tensor(z[:, 0:w], z[:, 0:w], z[:, w:2 * w], ALU.add))
                pool.tensor_tensor(acc[:, t, :], acc[:, t, :], z[:, 0:D], ALU.add).then_inc(mixture_added, 1)

            def add_exps(b, n, k):
                j = n % BLOCKS
                if j == 0:
                    return
                at = slice(0, b.sum_pool[n // BLOCKS])
                to = sums[:, (n // BLOCKS) % 2, at]
                wait_pair(pool, exp_done, b, STEPS, n + 1, k)
                if j == 1:
                    wait_pair(pool, o_ready, b, CHUNKS, n // BLOCKS - 1, k)
                else:
                    wait_pair(pool, summed_pool, b, CHUNKS * (BLOCKS - 1), sum_count(n - 1), k)
                pool.tensor_tensor(to, to if j > 1 else probs[:, (n - 1) % EXP_SLOTS, at],
                                   probs[:, n % EXP_SLOTS, at], ALU.add).then_inc(summed_pool, 1)

            def body(b, k=None):
                for n in range(STEPS):
                    if b.main:
                        add_exps(b, n, k)
                    for c in range(CHUNKS):
                        if b.prep and n == PREP_STRIDE * c + ROPE_AT - (AHEAD if c and b is first else 0):
                            rope(b, c, k)
                    if b is first and n == ADD_BIAS_AT:
                        pool.wait_ge(bo_here, 16)
                        pool.wait_ge(var_ready, CHUNKS)
                        chain(pool.tensor_tensor(acc[:, :, :], acc[:, :, :],
                                                 bo[:, None, :].to_broadcast([P, BLOCKS, D]), ALU.add))
                    if b is first and n - 1 in WEIGH_AT:
                        add_up(WEIGH_AT[n - 1])

            chain(pool.memset(ones[:, :], 1.0))
            for s in range(2):
                for h in range(2):
                    rows = (slice(DH, P), slice(0, DH))[h]
                    chain(pool.memset(q2[s][h][rows, :].bitcast(F32), 0.0))
                    chain(pool.memset(k2[s][h][rows, :].bitcast(F32), 1.0))
            pool.sem_inc(consts_set, 1)
            wait_ring(pool, first, ("act", 0), None)
            body(first)
            body(b0)
            with pool.Fori(0, ROUNDS) as k:
                body(odd, k)
                body(even, k)
            body(last)


def kernel(L0_attn_x, L0_attn_w_qkv, L0_attn_w_fproj, L0_attn_b_fproj, L0_attn_w_out, L0_attn_b_out,
           L0_ffn_w_router, L0_ffn_w_gate, L0_ffn_w_down):
    import concourse.bacc as bacc
    from concourse.bass_utils import run_bass_kernel_spmd

    f = np.float32
    pos = np.arange(N, dtype=f)[:, None]
    freqs = f(10000.0) ** (-np.arange(0, DH, 2, dtype=f) / f(DH))
    angles = (pos * freqs.astype(f)).astype(f)
    sin = np.repeat(np.sin(angles), 2, axis=1).astype(f)
    cos = np.repeat(np.cos(angles), 2, axis=1).astype(f)
    sin[:, :DH // 2] *= -1
    four = pos * np.arange(1, FREQS + 1, dtype=f)
    fourier = np.concatenate([np.sin(four), np.cos(four), np.ones((N, 1), f)], 1).T.astype(f)

    def tokens(a):
        return np.ascontiguousarray(np.asarray(a).reshape(BLOCKS, P, -1).transpose(1, 0, 2))

    w_fproj = np.concatenate([np.asarray(L0_attn_w_fproj).T, np.asarray(L0_attn_b_fproj)[None]], 0)
    w_qkv = np.asarray(L0_attn_w_qkv).reshape(3, PAIRS, P, D).transpose(1, 3, 0, 2).reshape(PAIRS, D, 3 * P)
    arrays = {
        "x": tokens(L0_attn_x),
        "w_qkv": np.concatenate([w_qkv, w_qkv[:1]]),
        "w_fproj": w_fproj,
        "w_out": np.asarray(L0_attn_w_out).T.reshape(PAIRS, P, D),
        "b_out": np.asarray(L0_attn_b_out)[None],
        "w_router": np.asarray(L0_ffn_w_router).T,
        "w_gate": np.asarray(L0_ffn_w_gate).T,
        "w_down": np.asarray(L0_ffn_w_down).reshape(EXPERTS, D, 2, P).transpose(3, 2, 0, 1).reshape(P, 2, EXPERTS * D),
        "cos": tokens(cos),
        "sin": tokens(sin),
        "fourier": fourier,
        "ident": np.eye(P, dtype=f),
        "tri": np.triu(np.ones((P, P), f)),
        "lower": np.tril(np.ones((EXPERTS, EXPERTS), f), -1).reshape(1, -1),
    }
    nc = bacc.Bacc("TRN2", target_bir_lowering=False, num_devices=1)
    feeds, args = {}, []
    for name, a in arrays.items():
        a = np.ascontiguousarray(a)
        feeds[f"in_{name}"] = a
        args.append(nc.dram_tensor(f"in_{name}", a.shape, mybir.dt.from_np(a.dtype), kind="ExternalInput").ap())
    out = nc.dram_tensor("out", (P, BLOCKS, D), F32, kind="ExternalOutput").ap()
    attention_and_mixture(nc, *args, out)
    got = run_bass_kernel_spmd(nc, [feeds], core_ids=[0]).results[0]["out"]
    return np.asarray(got).transpose(1, 0, 2).reshape(1, N, D)
```
